# Optimizing a Trainium2 kernel written in Bass

```python
import numpy as np
import jax
import jax.numpy as jnp

def _softmax(x, axis=-1):
    return jax.nn.softmax(x, axis=axis)
def _gelu(x):
    return jax.nn.gelu(x, approximate=True)
def _silu(x):
    return jax.nn.silu(x)
def _sigmoid(x):
    return jax.nn.sigmoid(x)
def _layernorm(x, axis=-1, eps=1e-5):
    m = jnp.mean(x, axis=axis, keepdims=True)
    v = jnp.var(x, axis=axis, keepdims=True)
    return (x - m) / jnp.sqrt(v + eps)
def _scatter_add(tgt, idx, src, axis=0):
    return tgt.at[idx].add(src)
def _segment_sum(src, seg, n):
    return jax.ops.segment_sum(src, seg, n)

kernel_name = 'mk_conv_preact_d2_conv_nhwc64_81653b'

def setup_inputs(seed: int = 0):
    np.random.seed(seed)
    _w = jnp.asarray
    def _rec_inputs():
        import jax
        import jax.numpy as jnp
        _gk = jax.random.key(seed)
        x = -0.000125 + 0.9999 * jax.random.normal(jax.random.fold_in(_gk, 1), (8, 256, 256, 64), jnp.float32)
        return x
    x = _rec_inputs()
    def _L0_conv_setup():
        import jax, jax.numpy as jnp
        import numpy as np
        B, H, W, C = (8, 256, 256, 64)
        M1, M2 = (32, 32)
        SCALE = 1.0 / (C * C)

        def _compl_mul2d(inp, weights):
            return jnp.einsum('bxyi,ioxy->bxyo', inp, weights)
        key = jax.random.key(seed)
        ku, k1, k2, k3, k4 = jax.random.split(key, 5)
        u = jax.random.normal(ku, (B, H, W, C), dtype=jnp.float32)
        wshape = (C, C, M1, M2)
        w_pos_r = SCALE * jax.random.normal(k1, wshape, dtype=jnp.float32)
        w_pos_i = SCALE * jax.random.normal(k2, wshape, dtype=jnp.float32)
        w_neg_r = SCALE * jax.random.normal(k3, wshape, dtype=jnp.float32)
        w_neg_i = SCALE * jax.random.normal(k4, wshape, dtype=jnp.float32)
        return {'u': u, 'w_pos_r': w_pos_r, 'w_pos_i': w_pos_i, 'w_neg_r': w_neg_r, 'w_neg_i': w_neg_i}
    _L0_conv_all = _L0_conv_setup()
    _L0_conv_in = {k: v for k, v in _L0_conv_all.items() if k in ('w_pos_r', 'w_pos_i', 'w_neg_r', 'w_neg_i', )}
    del _L0_conv_all

    def _L1_conv_setup():
        import jax, jax.numpy as jnp
        import numpy as np
        from jax import lax
        N, H, W, C_IN = (16, 112, 112, 64)
        C_OUT, KSIZE, STRIDE, PAD = (64, 3, 1, 1)
        key = jax.random.key(seed)
        kx, kw = jax.random.split(key)
        x = jax.random.normal(kx, (N, H, W, C_IN), dtype=jnp.float32)
        fan_in = KSIZE * KSIZE * C_IN
        fan_out = KSIZE * KSIZE * C_OUT
        std = np.sqrt(2.0 / (fan_in + fan_out)).astype(np.float32)
        kernels = jax.random.normal(kw, (C_OUT, KSIZE, KSIZE, C_IN), dtype=jnp.float32) * std
        return {'x': x, 'kernels': kernels, 'mode': 0}
    _L1_conv_all = _L1_conv_setup()
    _L1_conv_in = {k: v for k, v in _L1_conv_all.items() if k in ('kernels', )}
    del _L1_conv_all

    return {
        "x": x,
        "L0_conv_w_pos_r": _L0_conv_in["w_pos_r"],
        "L0_conv_w_pos_i": _L0_conv_in["w_pos_i"],
        "L0_conv_w_neg_r": _L0_conv_in["w_neg_r"],
        "L0_conv_w_neg_i": _L0_conv_in["w_neg_i"],
        "L1_conv_kernels": _L1_conv_in["kernels"],
    }

def reference(x, L0_conv_w_pos_r, L0_conv_w_pos_i, L0_conv_w_neg_r, L0_conv_w_neg_i, L1_conv_kernels):
    import jax
    import jax.numpy as jnp
    def _L0_conv_ref(u, w_pos_r, w_pos_i, w_neg_r, w_neg_i):
        import jax, jax.numpy as jnp
        import numpy as np
        B, H, W, C = (8, 256, 256, 64)
        M1, M2 = (32, 32)
        SCALE = 1.0 / (C * C)

        def _compl_mul2d(inp, weights):
            return jnp.einsum('bxyi,ioxy->bxyo', inp, weights)
        b, h, w, c = u.shape
        wf = w // 2 + 1
        u_ft = jnp.fft.rfft2(u, axes=(1, 2))
        w_pos = jax.lax.complex(w_pos_r, w_pos_i)
        w_neg = jax.lax.complex(w_neg_r, w_neg_i)
        top = _compl_mul2d(u_ft[:, :M1, :M2, :], w_pos)
        bot = _compl_mul2d(u_ft[:, h - M1:, :M2, :], w_neg)
        out_ft = jnp.zeros((b, h, wf, c), dtype=u_ft.dtype)
        out_ft = out_ft.at[:, :M1, :M2, :].set(top)
        out_ft = out_ft.at[:, h - M1:, :M2, :].set(bot)
        return jnp.fft.irfft2(out_ft, s=(h, w), axes=(1, 2)).astype(u.dtype)

    def _L1_conv_ref(x, kernels, mode):
        import jax, jax.numpy as jnp
        import numpy as np
        from jax import lax
        N, H, W, C_IN = (16, 112, 112, 64)
        C_OUT, KSIZE, STRIDE, PAD = (64, 3, 1, 1)
        out = lax.conv_general_dilated(x, kernels, window_strides=(STRIDE, STRIDE), padding=[(PAD, PAD), (PAD, PAD)], dimension_numbers=('NHWC', 'OHWI', 'NHWC'))
        return out

    def _gn(v, G=32, eps=1e-5):
        B_, H_, W_, C_ = v.shape
        g = v.reshape(B_, H_, W_, G, C_ // G)
        m = jnp.mean(g, axis=(1, 2, 4), keepdims=True)
        s = jnp.var(g, axis=(1, 2, 4), keepdims=True)
        return ((g - m) / jnp.sqrt(s + eps)).reshape(v.shape)

    def _ln_c(v, eps=1e-6):
        m = jnp.mean(v, axis=-1, keepdims=True)
        s = jnp.var(v, axis=-1, keepdims=True)
        return (v - m) / jnp.sqrt(s + eps)

    def _ln_t(v, eps=1e-5):
        m = jnp.mean(v, axis=-1, keepdims=True)
        s = jnp.var(v, axis=-1, keepdims=True)
        return (v - m) / jnp.sqrt(s + eps)

    def _to_tokens(v):
        B_, H_, W_, C_ = v.shape
        return v.reshape(B_, H_ * W_, C_)
    def _from_tokens(t, like):
        return t.reshape(like.shape)

    x = x + _L0_conv_ref(_gn(x), L0_conv_w_pos_r, L0_conv_w_pos_i, L0_conv_w_neg_r, L0_conv_w_neg_i)
    x = x + _L1_conv_ref(_gn(x), L1_conv_kernels, 0)
    return x


_drawn_inputs = setup_inputs


def setup_inputs(seed=0):
    import zlib

    import numpy as np

    out = dict(_drawn_inputs(seed))
    spreads = {}
    factors = {'L0_conv_w_pos_r': 64.0,
     'L0_conv_w_pos_i': 64.0,
     'L0_conv_w_neg_r': 64.0,
     'L0_conv_w_neg_i': 64.0}
    for name, (base, spread) in spreads.items():
        noise = np.random.default_rng([zlib.crc32(name.encode()), seed]).standard_normal(out[name].shape)
        drawn = base * np.exp(spread * noise) if base else spread * noise
        out[name] = jnp.asarray(drawn.astype(out[name].dtype))
    for name, factor in factors.items():
        out[name] = (out[name] * factor).astype(out[name].dtype)
    return out
```

```python
import numpy as np
import concourse.bass as bass
from concourse import mybir
from contextlib import ExitStack

F32 = mybir.dt.float32
F32R = mybir.dt.float32r
F16 = mybir.dt.float16
ALU = mybir.AluOpType
ACT = mybir.ActivationFunctionType
AX = mybir.AxisListType

P = 128
B, H, W, C = 8, 256, 256, 64
NKX, NKY = 64, 32
NPIX = H * W
GRP = 2
NORM = float(GRP * NPIX)
EPS = 1e-5
RC = 16
CPI = H // RC
NCH = B * CPI
GIVEN = 1
WSCALE = 8192.0

CW = {}
_at = 0
for _name, _n in (("fw", 2 * 64), ("fh", 4 * 128), ("eh", 256), ("fi", 256), ("ident", 128),
                  ("pair_re", 128), ("pair_all", 128), ("diag2", 64), ("diag_top", 64), ("sgn", 1), ("sgnh", 1)):
    CW[_name] = (_at, _at + _n)
    _at += _n
NCONST = _at


def constants():
    cst = np.zeros((P, NCONST), np.float64)

    def put(name, a):
        cst[:, CW[name][0]:CW[name][1]] = np.asarray(a).reshape(P, -1)

    turn = 2 * np.pi / W
    p, ky, j = np.arange(P), np.arange(NKY), np.arange(2)
    a = turn * ((2 * p[:, None, None] + j[None, :, None]) * ky[None, None, :] % W)
    put("fw", np.concatenate([np.cos(a), -np.sin(a)], -1))
    kx = np.arange(NKX)
    kx = np.where(kx < NKX // 2, kx, kx - NKX)
    h = (p[:, None] // 8) * 16 + p[:, None] % 8 + 8 * np.arange(2)[None, :]
    a = turn * (h[:, :, None] * kx[None, None, :] % H)
    re = np.concatenate([np.cos(a), -np.sin(a)], -1)
    im = np.concatenate([np.sin(a), np.cos(a)], -1)
    put("fh", np.stack([re, im], 2))
    a = turn * (kx[:, None] * np.arange(H)[None, :] % H)
    put("eh", np.concatenate([np.cos(a), -np.sin(a)], 0))
    w = np.concatenate([np.arange(1, W, 2), np.arange(0, W, 2)])
    a = turn * (ky[:, None] * w[None, :] % W)
    twice = np.where(ky == 0, 1.0, 2.0)[:, None] / NPIX
    f = np.concatenate([np.cos(a) * twice, -np.sin(a) * twice], 0)
    put("fi", np.concatenate([f, f], 0))
    put("ident", np.eye(P))
    k, m = np.arange(P)[:, None], np.arange(P)[None, :]
    same = (k % C) // GRP == (m % C) // GRP
    put("pair_re", same & (k < C))
    put("pair_all", same)
    put("diag2", (k % C == np.arange(C)[None, :]))
    put("diag_top", (k == np.arange(C)[None, :]))
    put("sgn", np.where(p < C, 1.0, -1.0))
    put("sgnh", np.where(p < C, 0.5, -0.5))
    return cst.astype(np.float32)


class Chain:

    def __init__(self, eng, sem, before, steps):
        self.eng, self.sem, self.before, self.steps, self.n = eng, sem, before, steps, 0

    def __call__(self, ins):
        self.n += 1
        ins.then_inc(self.sem, 1)
        self.eng.wait_ge(self.sem, self.before + self.n)

    def end(self):
        assert self.n == self.steps, self.n


def program(nc, x, w_pos_r, w_pos_i, w_neg_r, w_neg_i, ker, cst_in, out):
    modes_x = nc.dram_tensor("modes_x", [B, P, NKX * NKY], F32, kind="Internal").ap()
    modes_o = nc.dram_tensor("modes_o", [3, B, NKX, NKY * C], F32, kind="Internal").ap()

    with ExitStack() as ctx:
        sb = lambda name, shape, dt=F32: ctx.enter_context(nc.sbuf_tensor(name, shape, dt))
        sem = lambda name: ctx.enter_context(nc.semaphore(name))
        ps = ctx.enter_context(nc.psum_tensor("ps", [P, 8, 512], F32))
        cst = sb("cst", [P, NCONST])
        con = lambda name: cst[:, CW[name][0]:CW[name][1]]
        ident = con("ident")
        ones = sb("ones", [P, P])
        halves = sb("halves", [P, P])
        taps = sb("taps", [P, 3, 4, C])
        w_sq = sb("w_sq", [P, 1])
        mean0 = sb("mean0", [P, B])
        dev0 = sb("dev0", [P, B])
        fi_hi = sb("fi_hi", [P, W], F32R)
        fi_lo = sb("fi_lo", [P, W], F32R)
        setup(nc, cst_in, ker, ps, cst, con, ones, halves, taps, w_sq, fi_hi, fi_lo)
        phase_a(nc, x, modes_x, ps, con, cst_in[0:1, 0:8], ident, ones, mean0, dev0)
        phase_m(nc, (w_pos_r, w_pos_i), (w_neg_r, w_neg_i), modes_x, modes_o, ps, con, cst_in[0:1, 0:8], dev0)
        phase_b(nc, x, out, modes_x, modes_o, ps, con, cst_in[0:1, 0:8], ident, ones, halves, taps, w_sq, mean0, dev0, fi_hi, fi_lo)


def setup(nc, cst_in, ker, ps, cst, con, ones, halves, taps, w_sq, fi_hi, fi_lo):
    with ExitStack() as ctx:
        kw = ctx.enter_context(nc.sbuf_tensor("kw", [C, 9, 2, C], F32))
        w_part = ctx.enter_context(nc.sbuf_tensor("w_part", [P, 1], F32))
        w_junk = ctx.enter_context(nc.sbuf_tensor("w_junk", [P, 3 * 4 * C], F32))
        sem = lambda name: ctx.enter_context(nc.semaphore(name))
        consts_in, kernels_in, filled, turned, squared, summed, split = map(
            sem, ("consts_in", "kernels_in", "filled", "turned", "w_squared", "w_summed", "fi_split"))
        block = ctx.enter_context(nc.Block())

        @block.sync
        def _(sync):
            sync.dma_start(cst[:, :], cst_in).then_inc(consts_in, 16)
            for r in range(2):
                sync.dma_start(kw[:, :, r, :], ker.rearrange("o y x i -> o (y x) i")).then_inc(kernels_in, 16)

        @block.tensor
        def _(pe):
            pe.wait_ge(consts_in, 16)
            pe.wait_ge(kernels_in, 32)
            ident64 = con("ident")[0:C, 0:C]
            for tap in range(9):
                last = nc.tensor.transpose(ps[:, tap // 8, (tap % 8) * C:(tap % 8 + 1) * C],
                                           kw[:, tap, :, :].rearrange("o r i -> o (r i)"), ident64)
            last.then_inc(turned, 1)
            pe.wait_ge(squared, 1)
            pe.wait_ge(filled, 2)
            nc.tensor.matmul(ps[:, 2, 0:1], halves[:, :], w_part[:, :], start=True, stop=True).then_inc(summed, 1)

        @block.vector
        def _(dve):
            nc.vector.memset(ones[:, :], 1.0).then_inc(filled, 1)
            nc.vector.memset(halves[:, :], 0.5).then_inc(filled, 1)
            nc.vector.memset(taps[:, :, :, :], 0.0).then_inc(filled, 1)
            dve.wait_ge(filled, 3)
            dve.wait_ge(turned, 1)
            for dx in range(3):
                for r in range(2):
                    for q in range(r, r + 3):
                        tap = (r + 2 - q) * 3 + dx
                        last = nc.vector.tensor_copy(taps[C * r:C * r + C, dx, q, :],
                                                     ps[C * r:C * r + C, tap // 8, (tap % 8) * C:(tap % 8 + 1) * C])
            last.then_inc(filled, 1)
            dve.wait_ge(filled, 4)
            flat = taps[:, :, :, :].rearrange("p a b c -> p (a b c)")
            nc.vector.scalar_tensor_tensor(w_junk[:, :], flat, 1.0, flat, ALU.mult, ALU.mult,
                                           accum_out=w_part[:, :]).then_inc(squared, 1)
            dve.wait_ge(consts_in, 16)
            nc.vector.tensor_copy(fi_hi[:, :], con("fi")).then_inc(split, 1)
            dve.wait_ge(split, 1)
            nc.vector.tensor_tensor(fi_lo[:, :], con("fi"), fi_hi[:, :].bitcast(F32), ALU.subtract)
            dve.wait_ge(summed, 1)
            nc.vector.tensor_copy(w_sq[:, :], ps[:, 2, 0:1])


def phase_a(nc, x, modes_x, ps, con, con_in, ident, ones, mean0, dev0):
    NX = 8
    CB = 4
    CG = 16
    KB = 8
    NTR, NHG, NKB = C // CB, C // CG, NKY // KB
    x_v = x.rearrange("b (n r) (p j) c -> (b n) p r (j c)", r=RC, j=2)
    with ExitStack() as ctx:
        sb = lambda name, shape, dt=F32: ctx.enter_context(nc.sbuf_tensor(name, shape, dt))
        sem = lambda name: ctx.enter_context(nc.semaphore(name))
        xt = sb("a_xt", [P, NX, RC, 2 * C])
        sq = sb("a_sq", [P, 2, RC * 2 * C])
        acc = sb("a_acc", [P, RC * 2 * C])
        red = sb("a_red", [P, C // GRP])
        red4 = sb("a_red4", [P, 2, C // GRP, GRP])
        gw = sb("a_gw", [P, C, P])
        gh = sb("a_gh", [P, C, P])
        xh = sb("a_xh", [P, NKY, C])
        xc = sb("a_xc", [P, NKX, NKY])
        tmp = sb("a_tmp", [P, 8])
        seed = sb("a_seed", [1, 8])
        x_in = [sem(f"x_in{u}") for u in range(NX)]
        dft_done, dft_evac = sem("dft_done"), sem("dft_evac")
        sq_done, sq_used = sem("sq_done"), sem("sq_used")
        turned, gh_evac = sem("gw_turned"), sem("gh_evac")
        hdft_done, xh_evac = sem("hdft_done"), sem("xh_evac")
        mode_turned, xc_evac = sem("mode_turned"), sem("xc_evac")
        red_ready, sums_done, stats_step = sem("red_ready"), sem("sums_done"), sem("stats_step")
        xc_ready, xc_stored = sem("xc_ready"), sem("xc_stored")
        acc_summed, acc_cleared = sem("acc_summed"), sem("acc_cleared")
        block = ctx.enter_context(nc.Block())
        STATS = 6
        fw = con("fw").rearrange("p (j k) -> p j k", j=2)
        fh = con("fh").rearrange("p (g f k) -> p g f k", g=2, f=2)

        @block.sync
        def _(sync):
            def load(n, u):
                for half in (slice(0, RC // 2), slice(RC // 2, RC)):
                    sync.dma_start(xt[:, u, half, :], x_v[n][:, half]).then_inc(x_in[u], 16)

            for u in range(NX):
                load(u, u)
            with sync.Fori(0, NCH // NX - 1) as t:
                for u in range(NX):
                    sync.wait_ge(dft_done, t * NX + (u + 1))
                    sync.wait_ge(sq_done, t * NX + (u + 1))
                    load(t * NX + (u + NX), u)

        @block.tensor
        def _(pe):
            with pe.Fori(0, B) as b:
                with pe.Fori(0, CPI // NX) as t:
                    for u in range(NX):
                        pe.wait_ge(x_in[u], (b * (CPI // NX) + t) * 32 + 32)
                        pe.wait_ge(dft_evac, b * CPI + t * NX + (u + 1))
                        for j in range(2):
                            for g in range(2):
                                last = nc.tensor.matmul(ps[64 * g:64 * g + 64, u % 2, :], fw[:, j, :],
                                                        xt[:, u, 8 * g:8 * g + 8, C * j:C * j + C],
                                                        start=(j == 0), stop=(j == 1))
                        last.then_inc(dft_done, 1)
                pe.wait_ge(dft_evac, b * CPI + (CPI + 2))
                for q in range(NTR):
                    pe.wait_ge(gh_evac, b * NTR + (q + 1))
                    for i in range(CB):
                        last = nc.tensor.transpose(ps[:, 2 + q % 2, i * P:(i + 1) * P], gw[:, CB * q + i, :], ident)
                    last.then_inc(turned, 1)
                for q in range(NHG):
                    pe.wait_ge(gh_evac, b * NTR + ((q + 1) * CG // CB + 2))
                    pe.wait_ge(xh_evac, b * NHG + (q + 1))
                    for n, (g, f) in enumerate(((0, 0), (0, 1), (1, 0), (1, 1))):
                        lo = 64 * g + 32 * f
                        last = nc.tensor.matmul(ps[:, 4 + q % 2, :], fh[:, g, f, :],
                                                gh[:, CG * q:CG * (q + 1), lo:lo + NKY], start=(n == 0), stop=(n == 3))
                    last.then_inc(hdft_done, 1)
                pe.wait_ge(xh_evac, b * NHG + (NHG + 2))
                pe.wait_ge(red_ready, b + 1)
                for q in range(NKB):
                    pe.wait_ge(xc_evac, b * NKB + (q + 1))
                    for i in range(KB // 2):
                        ky = KB * q + 2 * i
                        last = nc.tensor.transpose(ps[:, 6 + q % 2, i * P:(i + 1) * P],
                                                   xh[:, ky:ky + 2, :].rearrange("p y c -> p (y c)"), ident)
                    last.then_inc(mode_turned, 1)
                pe.wait_ge(xc_evac, b * NKB + (NKB + 2))
                nc.tensor.matmul(ps[:, 6, 0:1], red4[:, :, :, :].rearrange("p a g e -> p (a g e)"),
                                 ones[:, 0:1], start=True, stop=True)
                nc.tensor.matmul(ps[:, 6, 1:2], con("pair_re"), xc[:, 0, 0:1],
                                 start=True, stop=True).then_inc(sums_done, 1)

        @block.scalar
        def _(act):
            with act.Fori(0, B) as b:
                with act.Fori(0, CPI // NX) as t:
                    for u in range(NX):
                        act.wait_ge(x_in[u], (b * (CPI // NX) + t) * 32 + 32)
                        act.wait_ge(sq_used, b * CPI + t * NX + (u + 1))
                        nc.scalar.activation(sq[:, u % 2, :], xt[:, u, :, :].rearrange("p r e -> p (r e)"),
                                             ACT.Square).then_inc(sq_done, 1)
                act.wait_ge(hdft_done, b * NHG + GIVEN)
                for q in range(NTR):
                    act.wait_ge(turned, b * NTR + (q + 1) + GIVEN)
                    nc.scalar.activation(gh[:, CB * q:CB * (q + 1), :].rearrange("p c k -> p (c k)"),
                                         ps[:, 2 + q % 2, :], ACT.Copy).then_inc(gh_evac, 1)
                act.wait_ge(xc_stored, b * 16 + 16)
                for q in range(NKB):
                    act.wait_ge(mode_turned, b * NKB + (q + 1) + GIVEN)
                    bank = ps[:, 6 + q % 2, :].rearrange("p (y f k) -> p f k y", y=KB // 2, f=2)
                    for f in range(2):
                        for e in range(2):
                            last = nc.scalar.activation(xc[C * f:C * f + C, :, KB * q + e:KB * (q + 1):2],
                                                        bank[C * e:C * e + C, f, :, :], ACT.Copy)
                    last.then_inc(xc_evac, 1)

        @block.vector
        def _(dve):
            nc.vector.memset(tmp[:, 0:1], 0.0).then_inc(dft_evac, 2)
            nc.vector.memset(tmp[:, 1:2], 0.0).then_inc(sq_used, 2)
            nc.vector.memset(tmp[:, 2:3], 0.0).then_inc(gh_evac, 2)
            nc.vector.memset(tmp[:, 3:4], 0.0).then_inc(xh_evac, 2)
            nc.vector.memset(red[:, :], 0.0).then_inc(xc_evac, 2)
            for i, s in enumerate((hdft_done, turned, sums_done, mode_turned)):
                nc.vector.memset(tmp[:, 4 + i:5 + i], 0.0).then_inc(s, GIVEN)
            nc.vector.memset(acc[:, :], 0.0).then_inc(acc_cleared, 1)
            with dve.Fori(0, B) as b:
                with dve.Fori(0, CPI // NX) as t:
                    for u in range(NX):
                        if u == 0:
                            dve.wait_ge(turned, b * NTR + GIVEN)
                            dve.wait_ge(acc_cleared, b + 1)
                        dve.wait_ge(dft_done, b * CPI + t * NX + (u + 1))
                        nc.vector.tensor_copy(gw[:, :, bass.ds(t * (8 * NX) + 8 * u, 8)],
                                              ps[:, u % 2, :].rearrange("p (r c) -> p c r", c=C)).then_inc(dft_evac, 1)
                        dve.wait_ge(sq_done, b * CPI + t * NX + (u + 1))
                        dve.wait_ge(sq_used, b * CPI + t * NX + (u + 2))
                        nc.vector.tensor_tensor(acc[:, :], acc[:, :], sq[:, u % 2, :], ALU.add).then_inc(sq_used, 1)
                dve.wait_ge(sq_used, b * CPI + (CPI + 2))
                dve.wait_ge(sums_done, b + GIVEN)
                nc.vector.tensor_reduce(red[:, :], acc[:, :].rearrange("p (m g e) -> p g m e", g=C // GRP, e=GRP),
                                        AX.XY, ALU.add).then_inc(acc_summed, 1)
                dve.wait_ge(acc_summed, b + 1)
                nc.vector.memset(acc[:, :], 0.0).then_inc(acc_cleared, 1)
                nc.vector.tensor_copy(red4[:, :, :, :],
                                      red[:, :].unsqueeze(1).unsqueeze(3).broadcast_to([P, 2, C // GRP, GRP]))\
                    .then_inc(red_ready, 1)
                dve.wait_ge(mode_turned, b * NKB + GIVEN)
                for q in range(NHG):
                    dve.wait_ge(hdft_done, b * NHG + (q + 1) + GIVEN)
                    nc.vector.tensor_copy(xh[:, :, CG * q:CG * (q + 1)],
                                          ps[:, 4 + q % 2, :].rearrange("p (c y) -> p y c", c=CG)).then_inc(xh_evac, 1)
                dve.wait_ge(sums_done, b + 1 + GIVEN)
                step = Chain(dve, stats_step, b * STATS, STATS)
                step(nc.vector.tensor_copy(tmp[:, 0:2], ps[:, 6, 0:2]))
                step(nc.vector.tensor_scalar(mean0[:, bass.ds(b, 1)], tmp[:, 1:2], 1.0 / NORM, None, ALU.mult))
                step(nc.vector.tensor_tensor(tmp[:, 2:3], tmp[:, 1:2], mean0[:, bass.ds(b, 1)], ALU.mult))
                step(nc.vector.tensor_tensor(dev0[:, bass.ds(b, 1)], tmp[:, 0:1], tmp[:, 2:3], ALU.subtract))
                step(nc.vector.tensor_scalar(tmp[:, 3:4], mean0[:, bass.ds(b, 1)], float(-NPIX), None, ALU.mult))
                step(nc.vector.tensor_tensor(xc[0:C, 0, 0:1], xc[0:C, 0, 0:1], tmp[0:C, 3:4], ALU.add))
                step.end()
                nc.vector.memset(tmp[:, 2:3], 0.0).then_inc(xc_ready, 1)

        @block.gpsimd
        def _(pool):
            pool.dma_start(seed[:, :], con_in).then_inc(xc_stored, 16)
            with pool.Fori(0, B) as b:
                pool.wait_ge(xc_ready, b + 1)
                pool.dma_start(modes_x[b], xc[:, :, :].rearrange("p k y -> p (k y)")).then_inc(xc_stored, 16)
            pool.wait_ge(xc_stored, B * 16 + 16)


def phase_m(nc, w_pos, w_neg, modes_x, modes_o, ps, con, con_in, dev0):
    KC = 4
    NM = NKX // KC
    MC = KC * NKY
    TQ = 4
    KT = NKY // TQ
    with ExitStack() as ctx:
        sb = lambda name, shape, dt=F32: ctx.enter_context(nc.sbuf_tensor(name, shape, dt))
        sem = lambda name: ctx.enter_context(nc.semaphore(name))
        wt = sb("m_w", [P, 2, C, MC])
        xs = sb("m_x", [P, 2, B, MC])
        st = sb("m_s", [P, 2, MC, 4 * B])
        ot = sb("m_o", [P, 2, KC, KT * C])
        seed = sb("m_seed", [1, 2, 8])
        rstd = sb("m_rstd", [P, 6, B])
        w_in = [sem(f"w_in{u}") for u in range(2)]
        xs_in = [sem(f"xs_in{u}") for u in range(2)]
        s_ready, o_done, o_evac, norm_step = sem("s_ready"), sem("o_done"), sem("o_evac"), sem("norm_step")
        var_ready, sqrt_done = sem("m_var_ready"), sem("m_sqrt_done")
        o_stored = [sem(f"o_stored{u}") for u in range(2)]
        block = ctx.enter_context(nc.Block())
        xs_v = modes_x.rearrange("b p (m e) -> m p b e", e=MC)
        w_v = [[w.rearrange("i o (m k) y -> m i o (k y)", k=KC) for w in pair] for pair in (w_pos, w_neg)]
        o_v = modes_o.rearrange("q b (m k) (t e) -> m t (q b) k e", k=KC, t=TQ)
        HALF = NM // 2

        @block.sync
        def _(sync):
            def load(sign, m_half, m, u):
                for ri in range(2):
                    sync.dma_start(wt[C * ri:C * ri + C, u, :, :], w_v[sign][ri][m_half]).then_inc(w_in[u], 16)
                sync.dma_start(xs[:, u, :, :], xs_v[m]).then_inc(xs_in[u], 16)

            for u in range(2):
                load(0, u, u, u)
            with sync.Fori(0, HALF // 2 - 1) as t:
                for u in range(2):
                    sync.wait_ge(o_done, t * (2 * KC) + (KC * (u + 1) + KC) + GIVEN)
                    load(0, t * 2 + (u + 2), t * 2 + (u + 2), u)
            with sync.Fori(0, HALF // 2) as t:
                for u in range(2):
                    sync.wait_ge(o_done, t * (2 * KC) + (KC * (HALF + u - 1) + KC) + GIVEN)
                    load(1, t * 2 + u, t * 2 + (HALF + u), u)

        @block.tensor
        def _(pe):
            with pe.Fori(0, NM // 2) as t:
                for u in range(2):
                    pe.wait_ge(w_in[u], t * 32 + 32)
                    pe.wait_ge(s_ready, t * 2 + (u + 1))
                    for k in range(KC):
                        pe.wait_ge(o_evac, t * (2 * KC) + (KC * u + k + 1))
                        for i in range(KT):
                            for tq in range(TQ):
                                mode = k * NKY + tq * KT + i
                                last = nc.tensor.matmul(ps[32 * tq:32 * tq + 32, KC * u + k, C * i:C * i + C],
                                                        st[:, u, mode, :], wt[:, u, :, mode], start=True, stop=True)
                        last.then_inc(o_done, 1)

        @block.vector
        def _(dve):
            nc.vector.memset(rstd[:, 5, 0:1], 0.0).then_inc(o_done, KC + GIVEN)
            nc.vector.memset(rstd[:, 5, 1:2], 0.0).then_inc(o_evac, 8)
            step = Chain(dve, norm_step, 0, 10)
            step(nc.vector.memset(st[:, :, :, 3 * B:], 0.0))
            step(nc.vector.tensor_scalar(rstd[:, 3, :], dev0[:, :], 1.0 / NORM, 0.0, ALU.mult, ALU.max))
            step(nc.vector.tensor_scalar(rstd[:, 3, :], rstd[:, 3, :], EPS, None, ALU.add))
            nc.vector.memset(rstd[:, 5, 0:1], 0.0).then_inc(var_ready, 1)
            dve.wait_ge(sqrt_done, 1)
            step(nc.vector.reciprocal(rstd[:, 0, :], rstd[:, 4, :]))
            step(nc.vector.tensor_tensor(rstd[:, 0, :], rstd[:, 0, :], rstd[:, 3, :], ALU.mult))
            step(nc.vector.tensor_tensor(rstd[:, 0, :], rstd[:, 0, :], rstd[:, 4, :], ALU.add))
            step(nc.vector.tensor_scalar(rstd[:, 5, :], rstd[:, 0, :], 0.5, None, ALU.mult))
            step(nc.vector.reciprocal(rstd[:, 0, :], rstd[:, 5, :]))
            step(nc.vector.tensor_scalar(rstd[:, 1, :], rstd[:, 0, :], con("sgn"), None, ALU.mult))
            step(nc.vector.tensor_scalar(rstd[:, 2, :], rstd[:, 1, :], -1.0, None, ALU.mult))
            step.end()
            with dve.Fori(0, NM // 2) as t:
                for u in range(2):
                    dve.wait_ge(xs_in[u], t * 16 + 16)
                    dve.wait_ge(o_done, t * (2 * KC) + KC * u + GIVEN)
                    cols = lambda q: st[:, u, :, q * B:(q + 1) * B].rearrange("p m b -> p b m")
                    scale = lambda row: rstd[:, row, :].unsqueeze(2).broadcast_to([P, B, MC])
                    nc.vector.tensor_tensor(cols(0), xs[:, u, :, :], scale(1), ALU.mult)
                    nc.vector.tensor_tensor(cols(2), xs[:, u, :, :], scale(2), ALU.mult)
                    nc.vector.tensor_tensor(cols(1)[C:P], xs[0:C, u, :, :], scale(0)[0:C], ALU.mult)
                    nc.vector.tensor_tensor(cols(1)[0:C], xs[C:P, u, :, :], scale(0)[C:P], ALU.mult).then_inc(s_ready, 1)

        @block.scalar
        def _(act):
            for u in range(2):
                act.dma_start(seed[:, u, :], con_in).then_inc(o_stored[u], 16)
            act.wait_ge(var_ready, 1)
            nc.scalar.activation(rstd[:, 4, :], rstd[:, 3, :], ACT.Sqrt).then_inc(sqrt_done, 1)
            with act.Fori(0, NM // 2) as t:
                for u in range(2):
                    act.wait_ge(o_stored[u], t * 64 + 16)
                    for k in range(KC):
                        act.wait_ge(o_done, t * (2 * KC) + (KC * u + k + 1 + KC) + GIVEN)
                        nc.scalar.activation(ot[:, u, k, :], ps[:, KC * u + k, :], ACT.Copy).then_inc(o_evac, 1)
                    act.wait_ge(o_evac, t * (2 * KC) + (KC * u + KC + 8))
                    for tq in range(TQ):
                        act.dma_start(o_v[t * 2 + u, tq], ot[32 * tq:32 * tq + 3 * B, u, :, :]).then_inc(o_stored[u], 16)
            for u in range(2):
                act.wait_ge(o_stored[u], NM // 2 * 64 + 16)


def phase_b(nc, x, out, modes_x, modes_o, ps, con, con_in, ident, ones, halves, taps, w_sq, mean0, dev0, fi_hi, fi_lo):
    RB = 8
    NB = H // RB
    BB = 4
    NIT = NB // BB
    NY = H // 4
    RING = 16
    ZW = W + 4
    NOT = NKY // 8
    NTB = C // 4
    Y0, CV = 0, 4
    x_v = x.rearrange("b (n r) (p j) c -> b n p j r c", r=RC, j=2)
    out_v = out.rearrange("b (n r) (p j) c -> b n p r (j c)", r=RB, j=2)
    with ExitStack() as ctx:
        sb = lambda name, shape, dt=F32: ctx.enter_context(nc.sbuf_tensor(name, shape, dt))
        sem = lambda name: ctx.enter_context(nc.semaphore(name))
        om = sb("b_om", [P, 2, NKY, C])
        xm = sb("b_xm", [P, NKX, NKY])
        oc = sb("b_oc", [P, NKX, NKY])
        work = sb("b_work", [P, NKX * NKY])
        sc = sb("b_sc", [P, 32])
        th = sb("b_th", [P, H, C], F32R)
        ts = sb("b_ts", [P, 2, RC, C], F32R)
        xt = sb("b_xt", [P, 2, 2, RC, C])
        zh = sb("b_zh", [P, RING, ZW], F16)
        zl = sb("b_zl", [P, RING, ZW], F16)
        wf = sb("b_wf", [P, 3, 4, C])
        wh = sb("b_wh", [P, 3, 4, C], F16)
        wl = sb("b_wl", [P, 3, 4, C], F16)
        diag = sb("b_diag", [P, C])
        seed = sb("b_seed", [1, BB, 8])
        mrow = sb("b_mrow", [P, C])
        ob = sb("b_ob", [P, BB, RB, 2 * C])
        col = {n: sc[:, i:i + 1] for i, n in enumerate(
            ("a_rest", "a_ky0", "a_mirror", "a_dc", "part", "dc", "mean", "mean_d", "var", "sd", "sigma", "rstd",
             "w1", "w2", "fro", "froot", "f", "inv_f", "sigma_f", "w3"))}
        om_in, xm_in = sem("om_in"), sem("xm_in")
        x_in = [sem(f"bx_in{u}") for u in range(2)]
        oc_turned, oc_even, oc_odd = sem("oc_turned"), sem("oc_even"), sem("oc_odd")
        part_ready, group_done, var_ready, sd_ready = map(sem, ("part_ready", "group_done", "b_var_ready", "sd_ready"))
        sig_done, fro_ready, froot_ready = map(sem, ("sig_done", "fro_ready", "froot_ready"))
        w_ready, mean_ready, mrow_done, om_fixed = map(sem, ("w_ready", "mean_ready", "mrow_done", "om_fixed"))
        t_done, t_hi, t_lo, ts_ready = map(sem, ("t_done", "t_hi", "t_lo", "ts_ready"))
        y_done, z_hi, z_lo, conv_done, out_evac = map(sem, ("y_done", "z_hi", "z_lo", "conv_done", "out_evac"))
        out_stored = [sem(f"out_stored{u}") for u in range(BB)]
        bstep, cleared = sem("bstep"), sem("cleared")
        block = ctx.enter_context(nc.Block())
        YG = 8
        STEPS = 35

        @block.sync
        def _(sync):
            def load_x(b, n, u):
                for j in range(2):
                    sync.dma_start(xt[:, u, j, :, :], x_v[b, n][:, j]).then_inc(x_in[u], 16)

            def body(b, it, last=False):
                for kk in range(BB):
                    if kk % 2 == 0 and not last:
                        sync.wait_ge(y_done, b * NY + it * (2 * BB) + (2 * kk + 4 + YG))
                        load_x(b, it * 2 + (kk // 2 + 2), kk // 2)
                    sync.wait_ge(out_evac, b * (2 * NB) + it * (2 * BB) + 2 * (kk + 1) + GIVEN)
                    sync.dma_start(out_v[b, it * BB + kk], ob[:, kk, :, :]).then_inc(out_stored[kk], 16)

            for u in range(BB):
                sync.dma_start(seed[:, u, :], con_in).then_inc(out_stored[u], 16)
            with sync.Fori(0, B) as b:
                sync.wait_ge(t_done, b * NTB + GIVEN)
                for form in range(2):
                    for ri in range(2):
                        sync.dma_start(om[NKX * ri:NKX * ri + NKX, form, :, :].rearrange("p y o -> p (y o)"),
                                       modes_o[form + ri, b]).then_inc(om_in, 16)
                sync.wait_ge(part_ready, b + GIVEN)
                sync.dma_start(xm[:, :, :].rearrange("p k y -> p (k y)"), modes_x[b]).then_inc(xm_in, 16)
                sync.wait_ge(y_done, b * NY + YG)
                for u in range(2):
                    load_x(b, u, u)
                with sync.Fori(0, NIT - 1) as it:
                    body(b, it)
                body(b, NIT - 1, last=True)
            for u in range(BB):
                sync.wait_ge(out_stored[u], B * NIT * 16 + 16)

        @block.tensor
        def _(pe):
            def y_bank(b, it, n):
                u = (n // 4) % 2
                if n % 4 == 0:
                    uses = b * (CPI // 2) + it + (n // 8)
                    pe.wait_ge(x_in[u], uses * 32 + 32)
                    pe.wait_ge(ts_ready, b * CPI + it * 2 + (n // 4 + 1) + GIVEN)
                if isinstance(it, int) and 2 * BB * it + n < 4:
                    pe.wait_ge(t_lo, b * NTB + NTB)
                else:
                    pe.wait_ge(z_lo, b * NY + it * (2 * BB) + (n - 3) + GIVEN)
                bank = Y0 + n % 4
                for k in range(2):
                    r = (n % 4) * 4 + 2 * k
                    for jj in range(2):
                        j = 1 - jj
                        nc.tensor.matmul(ps[:, bank, k * W + jj * P:k * W + (jj + 1) * P],
                                         xt[:, u, j, r:r + 2, :].rearrange("p r c -> p (r c)"), ident, is_transpose=True,
                                         start=(k == 0 and jj == 0), stop=False, skip_group_check=True)
                for k in range(2):
                    r = (n % 4) * 4 + 2 * k
                    for f in (fi_hi, fi_lo):
                        last = nc.tensor.matmul(ps[:, bank, k * W:(k + 1) * W],
                                                ts[:, u, r:r + 2, :].rearrange("p r c -> p (r c)"), f[:, :],
                                                start=False, stop=(f is fi_lo and k == 1), skip_group_check=True)
                last.then_inc(y_done, 1)

            def conv_block(b, it, kk, first, last_block):
                k_done = b * NB + it * BB + kk
                pe.wait_ge(z_lo, b * NY + it * (2 * BB) + (2 * kk + (2 if last_block else 3)) + GIVEN)
                if first:
                    pe.wait_ge(w_ready, b + 1 + GIVEN)
                if isinstance(it, int) and BB * it + kk < 2:
                    pe.wait_ge(out_evac, b * (2 * NB) + GIVEN)
                else:
                    pe.wait_ge(out_evac, k_done * 2 - 2 + GIVEN)
                pairs = range(4 * kk - (0 if first else 1), 4 * kk + (4 if last_block else 5))
                for j in range(2):
                    bank = CV + 2 * (kk % 2) + j
                    n, total = 0, 9 * len(pairs)
                    for dx in range(3):
                        at = ((0, 1 + P, 1), (1 + P, 1, 2 + P))[j][dx]
                        for z, w in ((zh, wh), (zl, wh), (zh, wl)):
                            for pair in sorted(pairs, key=lambda q: not 4 * kk <= q < 4 * kk + 4):
                                row = 2 * pair - 1 - RB * kk
                                q0, q1 = max(0, -row), min(4, RB - row)
                                last = nc.tensor.matmul(
                                    ps[:, bank, (row + q0) * C:(row + q1) * C],
                                    z[:, pair % RING, at:at + P],
                                    w[:, dx, q0:q1, :].rearrange("p q o -> p (q o)"),
                                    start=(n == 0), stop=(n == total - 1), skip_group_check=True)
                                n += 1
                last.then_inc(conv_done, 1)

            def body(b, it, first=False, last=False):
                for kk in range(BB):
                    for n in (2 * kk + 3, 2 * kk + 4):
                        if not (last and n >= 2 * BB):
                            y_bank(b, it, n)
                    conv_block(b, it, kk, first and kk == 0, last and kk == BB - 1)

            with pe.Fori(0, B) as b:
                pe.wait_ge(om_in, b * 64 + 64)
                pe.wait_ge(z_lo, b * NY + GIVEN)
                for q in range(NOT):
                    for i in range(4):
                        ky = 8 * q + 2 * i
                        last = nc.tensor.transpose(ps[:, Y0 + q, i * P:(i + 1) * P],
                                                   om[:, 0, ky:ky + 2, :].rearrange("p y c -> p (y c)"), ident)
                    last.then_inc(oc_turned, 1)
                pe.wait_ge(out_evac, b * (2 * NB) + GIVEN)
                pe.wait_ge(part_ready, b + 1 + GIVEN)
                nc.tensor.matmul(ps[:, CV, 0:1], con("pair_all"), col["part"], start=True, stop=True)
                nc.tensor.matmul(ps[:, CV, 1:2], con("pair_re"), col["dc"], start=True, stop=True).then_inc(group_done, 1)
                pe.wait_ge(var_ready, b + 1)
                nc.tensor.matmul(ps[:, CV + 1, 0:1], halves[:, :], col["var"], start=True, stop=True).then_inc(sig_done, 1)
                pe.wait_ge(mean_ready, b + 1)
                nc.tensor.matmul(ps[:, CV + 2, 0:C], ones[:, :], diag[:, :], start=True, stop=True).then_inc(mrow_done, 1)
                pe.wait_ge(om_fixed, b + 1)
                for q in range(NTB):
                    if q < 4:
                        pe.wait_ge(oc_even, b * NOT + (q + 1))
                        pe.wait_ge(oc_odd, b * NOT + (q + 1))
                    else:
                        pe.wait_ge(t_lo, b * NTB + (q - 3))
                    for i in range(2):
                        for half in range(2):
                            c = 2 * q + i + half * (C // 2)
                            last = nc.tensor.matmul(ps[64 * half:64 * half + 64, Y0 + q % 4, i * H:(i + 1) * H],
                                                    om[:, :, :, c].rearrange("p f y -> p (f y)"), con("eh"),
                                                    start=True, stop=True)
                    last.then_inc(t_done, 1)
                for n in range(3):
                    y_bank(b, 0, n)
                body(b, 0, first=True)
                with pe.Fori(1, NIT - 1) as it:
                    body(b, it)
                body(b, NIT - 1, last=True)

        def z_slot(t, n):
            return t[:, (2 * n) % RING:(2 * n) % RING + 2, 1:1 + W]

        def y_order(nit_last):
            return [[n for n in (2 * kk + 3, 2 * kk + 4) if not (nit_last and n >= 2 * BB)] for kk in range(BB)]

        @block.scalar
        def _(act):
            def high(b, it, n, blocks):
                act.wait_ge(y_done, b * NY + it * (2 * BB) + (n + 1 + YG))
                act.wait_ge(conv_done, blocks + GIVEN)
                nc.scalar.activation(z_slot(zh, n), ps[:, Y0 + n % 4, :].rearrange("p (k w) -> p k w", k=2),
                                     ACT.Copy, scale=col["rstd"]).then_inc(z_hi, 1)

            def body(b, it, first=False, last=False):
                for kk, banks in enumerate(y_order(last)):
                    for n in banks:
                        high(b, it, n, b * NB if first and kk == 0 else b * NB + it * BB + (kk - 1))

            with act.Fori(0, B) as b:
                act.wait_ge(w_ready, b + GIVEN)
                for q in range(NOT):
                    act.wait_ge(oc_turned, b * NOT + (q + 1))
                    bank = ps[:, Y0 + q, :].rearrange("p (y f k) -> p f k y", y=4, f=2)
                    for f in range(2):
                        last = nc.scalar.activation(oc[C * f:C * f + C, :, 8 * q:8 * q + 8:2], bank[0:C, f, :, :], ACT.Copy)
                    last.then_inc(oc_even, 1)
                act.wait_ge(var_ready, b + 1)
                nc.scalar.activation(col["sd"], col["var"], ACT.Sqrt).then_inc(sd_ready, 1)
                act.wait_ge(fro_ready, b + 1)
                nc.scalar.activation(col["froot"], col["fro"], ACT.Sqrt).then_inc(froot_ready, 1)
                act.wait_ge(ts_ready, b * CPI + GIVEN)
                for q in range(NTB):
                    act.wait_ge(t_done, b * NTB + (q + 1) + GIVEN)
                    for half in range(2):
                        c = 2 * q + half * (C // 2)
                        last = nc.scalar.activation(
                            th[64 * half:64 * half + 64, :, c:c + 2],
                            ps[64 * half:64 * half + 64, Y0 + q % 4, :].rearrange("p (c h) -> p h c", c=2), ACT.Copy)
                    last.then_inc(t_hi, 1)
                act.wait_ge(w_ready, b + 1 + GIVEN)
                act.wait_ge(cleared, 1)
                for n in range(3):
                    high(b, 0, n, b * NB)
                body(b, 0, first=True)
                with act.Fori(1, NIT - 1) as it:
                    body(b, it)
                body(b, NIT - 1, last=True)

        @block.vector
        def _(dve):
            v = nc.vector

            def low(b, it, n):
                dve.wait_ge(z_hi, b * NY + it * (2 * BB) + (n + 1))
                v.scalar_tensor_tensor(z_slot(zl, n), ps[:, Y0 + n % 4, :].rearrange("p (k w) -> p k w", k=2),
                                       col["rstd"], z_slot(zh, n), ALU.mult, ALU.subtract).then_inc(z_lo, 1)

            def take(b, it, kk):
                dve.wait_ge(conv_done, b * NB + it * BB + (kk + 1) + GIVEN)
                dve.wait_ge(out_stored[kk], (b * NIT + it) * 16 + 16)
                for j in range(2):
                    v.scalar_tensor_tensor(ob[:, kk, :, C * j:C * j + C],
                                           ps[:, CV + 2 * (kk % 2) + j, :].rearrange("p (r o) -> p r o", o=C),
                                           col["inv_f"], mrow[:, :].unsqueeze(1).broadcast_to([P, RB, C]),
                                           ALU.mult, ALU.add).then_inc(out_evac, 1)

            def body(b, it, first=False, last=False):
                for kk, banks in enumerate(y_order(last)):
                    for n in banks:
                        low(b, it, n)
                    if not (first and kk == 0):
                        take(b, it - 1 if kk == 0 else it, (kk - 1) % BB)

            v.memset(sc[:, 23:24], 0.0).then_inc(y_done, YG)
            for i, s in enumerate((t_done, part_ready, z_lo, out_evac, w_ready, ts_ready, conv_done)):
                v.memset(sc[:, 24 + i:25 + i], 0.0).then_inc(s, GIVEN)
            for z in (zh, zl):
                v.memset(z[:, :, 0:1], 0.0)
                v.memset(z[:, :, 1 + W:], 0.0)
            v.memset(sc[:, 22:23], 0.0).then_inc(cleared, 1)
            with dve.Fori(0, B) as b:
                for q in range(NOT):
                    dve.wait_ge(oc_turned, b * NOT + (q + 1))
                    bank = ps[:, Y0 + q, :].rearrange("p (y f k) -> p f k y", y=4, f=2)
                    for f in range(2):
                        last = v.tensor_copy(oc[C * f:C * f + C, :, 8 * q + 1:8 * q + 8:2], bank[C:P, f, :, :])
                    last.then_inc(oc_odd, 1)
                dve.wait_ge(oc_even, b * NOT + NOT)
                dve.wait_ge(oc_odd, b * NOT + NOT)
                dve.wait_ge(xm_in, b * 16 + 16)
                step = Chain(dve, bstep, b * STEPS, STEPS)
                rest = work[:, 0:NKX * (NKY - 1)].rearrange("p (k y) -> p k y", k=NKX)
                ky0 = work[:, 0:NKX]
                step(v.scalar_tensor_tensor(rest, xm[:, :, 1:], 2.0, oc[:, :, 1:], ALU.mult, ALU.add))
                step(v.scalar_tensor_tensor(rest, rest, 1.0, oc[:, :, 1:], ALU.mult, ALU.mult, accum_out=col["a_rest"]))
                step(v.scalar_tensor_tensor(ky0, xm[:, :, 0], 4.0, oc[:, :, 0], ALU.mult, ALU.add))
                step(v.scalar_tensor_tensor(ky0, ky0, 1.0, oc[:, :, 0], ALU.mult, ALU.mult, accum_out=col["a_ky0"]))
                step(v.scalar_tensor_tensor(work[:, 0:31], oc[:, 1:32, 0], 2.0, oc[:, 63:32:-1, 0],
                                            ALU.mult, ALU.mult, accum_out=col["a_mirror"]))
                step(v.tensor_tensor(col["a_dc"], oc[:, 0, 0:1], oc[:, 0, 0:1], ALU.mult))
                step(v.tensor_tensor(col["w1"], col["a_mirror"], col["a_dc"], ALU.add))
                step(v.tensor_tensor(col["w1"], col["w1"], con("sgnh"), ALU.mult))
                step(v.scalar_tensor_tensor(col["w2"], col["a_ky0"], 0.5, col["w1"], ALU.mult, ALU.add))
                step(v.scalar_tensor_tensor(col["part"], col["a_rest"], 2.0, col["w2"], ALU.mult, ALU.add))
                step(v.tensor_tensor(col["dc"], oc[:, 0, 0:1], xm[:, 0, 0:1], ALU.add))
                v.memset(sc[:, 23:24], 0.0).then_inc(part_ready, 1)
                dve.wait_ge(group_done, b + 1)
                step(v.tensor_scalar(col["mean_d"], ps[:, CV, 1:2], 1.0 / NORM, None, ALU.mult))
                step(v.tensor_tensor(col["mean"], col["mean_d"], mean0[:, bass.ds(b, 1)], ALU.add))
                step(v.scalar_tensor_tensor(col["w1"], ps[:, CV, 0:1], 1.0 / NPIX, dev0[:, bass.ds(b, 1)], ALU.mult, ALU.add))
                step(v.tensor_tensor(col["w2"], col["mean_d"], col["mean_d"], ALU.mult))
                step(v.scalar_tensor_tensor(col["w1"], col["w1"], 1.0 / NORM, col["w2"], ALU.mult, ALU.subtract))
                step(v.tensor_scalar(col["var"], col["w1"], 0.0, EPS, ALU.max, ALU.add))
                v.tensor_scalar(diag[:, :], con("diag_top"), col["mean"], None, ALU.mult).then_inc(mean_ready, 1)
                v.memset(sc[:, 23:24], 0.0).then_inc(var_ready, 1)
                dve.wait_ge(mrow_done, b + 1)
                step(v.tensor_copy(mrow[:, :], ps[:, CV + 2, 0:C]))
                step(v.scalar_tensor_tensor(om[0:1, 0, 0, :], mrow[0:1, :], float(-NPIX), om[0:1, 0, 0, :], ALU.mult, ALU.add))
                step(v.scalar_tensor_tensor(om[NKX:NKX + 1, 1, 0, :], mrow[NKX:NKX + 1, :], float(NPIX),
                                            om[NKX:NKX + 1, 1, 0, :], ALU.mult, ALU.add))
                v.memset(sc[:, 23:24], 0.0).then_inc(om_fixed, 1)
                dve.wait_ge(sig_done, b + 1)
                step(v.tensor_tensor(col["fro"], ps[:, CV + 1, 0:1], w_sq[:, :], ALU.add))
                v.memset(sc[:, 23:24], 0.0).then_inc(fro_ready, 1)
                dve.wait_ge(sd_ready, b + 1)
                step(v.reciprocal(col["w1"], col["sd"]))
                step(v.tensor_tensor(col["w1"], col["w1"], col["var"], ALU.mult))
                step(v.tensor_tensor(col["w1"], col["w1"], col["sd"], ALU.add))
                step(v.tensor_scalar(col["sigma"], col["w1"], 0.5, None, ALU.mult))
                step(v.reciprocal(col["rstd"], col["sigma"]))
                dve.wait_ge(froot_ready, b + 1)
                step(v.reciprocal(col["w2"], col["froot"]))
                step(v.tensor_scalar(col["f"], col["w2"], WSCALE, None, ALU.mult))
                step(v.reciprocal(col["inv_f"], col["f"]))
                step(v.tensor_tensor(col["sigma_f"], col["sigma"], col["f"], ALU.mult))
                step(v.tensor_scalar(wf[:, :, :, :].rearrange("p a q o -> p (a q o)"),
                                     taps[:, :, :, :].rearrange("p a q o -> p (a q o)"), col["f"], None, ALU.mult))
                for r in range(2):
                    half = slice(C * r, C * r + C)
                    step(v.scalar_tensor_tensor(wf[half, 1, 1 + r, :], con("diag2")[half], col["sigma_f"][half],
                                                wf[half, 1, 1 + r, :], ALU.mult, ALU.add))
                dve.wait_ge(conv_done, b * NB + GIVEN)
                step(v.tensor_copy(wh[:, :, :, :].rearrange("p a q o -> p (a q o)"),
                                   wf[:, :, :, :].rearrange("p a q o -> p (a q o)")))
                step(v.tensor_tensor(wl[:, :, :, :], wf[:, :, :, :], wh[:, :, :, :], ALU.subtract))
                step.end()
                v.memset(sc[:, 23:24], 0.0).then_inc(w_ready, 1)
                for q in range(NTB):
                    dve.wait_ge(t_hi, b * NTB + (q + 1))
                    for half in range(2):
                        c = 2 * q + half * (C // 2)
                        mine, other = slice(64 * half, 64 * half + 64), slice(64 * (1 - half), 64 * (1 - half) + 64)
                        last = v.tensor_tensor(th[other, :, c:c + 2],
                                               ps[mine, Y0 + q % 4, :].rearrange("p (c h) -> p h c", c=2),
                                               th[mine, :, c:c + 2].bitcast(F32), ALU.subtract)
                    last.then_inc(t_lo, 1)
                for n in range(3):
                    low(b, 0, n)
                body(b, 0, first=True)
                with dve.Fori(1, NIT - 1) as it:
                    body(b, it)
                body(b, NIT - 1, last=True)
                take(b, NIT - 1, BB - 1)

        @block.gpsimd
        def _(pool):
            with pool.Fori(0, B) as b:
                with pool.Fori(0, CPI // 2) as t:
                    for u in range(2):
                        pool.wait_ge(t_lo, b * NTB + NTB)
                        pool.wait_ge(y_done, b * NY + t * 8 + (4 * u + 4))
                        nc.gpsimd.tensor_copy(ts[:, u, :, :], th[:, bass.ds(t * (2 * RC) + RC * u, RC), :].bitcast(F32))\
                            .then_inc(ts_ready, 1)


_INS = ["x", "L0_conv_w_pos_r", "L0_conv_w_pos_i", "L0_conv_w_neg_r", "L0_conv_w_neg_i", "L1_conv_kernels"]


def kernel(**inputs):
    import concourse.bacc as bacc
    from concourse.bass_utils import run_bass_kernel_spmd

    nc = bacc.Bacc("TRN2", target_bir_lowering=False, num_devices=1)
    arrays, args = {}, []
    for name in _INS:
        arrays[name] = np.ascontiguousarray(inputs[name])
    arrays["constants"] = constants()
    for name, a in arrays.items():
        args.append(nc.dram_tensor(name, a.shape, mybir.dt.from_np(a.dtype), kind="ExternalInput").ap())
    out = nc.dram_tensor("out", (B, H, W, C), F32, kind="ExternalOutput").ap()
    program(nc, *args, out)
    r = run_bass_kernel_spmd(nc, [arrays], core_ids=[0])
    return r.results[0]["out"]
```

```python
import numpy as np
import concourse.bass as bass
from concourse import mybir
from contextlib import ExitStack

F32 = mybir.dt.float32
F32R = mybir.dt.float32r
F16 = mybir.dt.float16
ALU = mybir.AluOpType
ACT = mybir.ActivationFunctionType
AX = mybir.AxisListType

P = 128
B, H, W, C = 8, 256, 256, 64
NKX, NKY = 64, 32
NPIX = H * W
GRP = 2
NORM = float(GRP * NPIX)
EPS = 1e-5
RC = 16
CPI = H // RC
NCH = B * CPI
GIVEN = 1
WSCALE = 8192.0

CW = {}
_at = 0
for _name, _n in (("fw", 2 * 64), ("fh", 4 * 128), ("eh", 256), ("fi", 256), ("ident", 128),
                  ("pair_re", 128), ("pair_all", 128), ("diag2", 64), ("diag_top", 64), ("sgn", 1), ("sgnh", 1)):
    CW[_name] = (_at, _at + _n)
    _at += _n
NCONST = _at


def constants():
    cst = np.zeros((P, NCONST), np.float64)

    def put(name, a):
        cst[:, CW[name][0]:CW[name][1]] = np.asarray(a).reshape(P, -1)

    turn = 2 * np.pi / W
    p, ky, j = np.arange(P), np.arange(NKY), np.arange(2)
    a = turn * ((2 * p[:, None, None] + j[None, :, None]) * ky[None, None, :] % W)
    put("fw", np.concatenate([np.cos(a), -np.sin(a)], -1))
    kx = np.arange(NKX)
    kx = np.where(kx < NKX // 2, kx, kx - NKX)
    h = (p[:, None] // 8) * 16 + p[:, None] % 8 + 8 * np.arange(2)[None, :]
    a = turn * (h[:, :, None] * kx[None, None, :] % H)
    re = np.concatenate([np.cos(a), -np.sin(a)], -1)
    im = np.concatenate([np.sin(a), np.cos(a)], -1)
    put("fh", np.stack([re, im], 2))
    a = turn * (kx[:, None] * np.arange(H)[None, :] % H)
    put("eh", np.concatenate([np.cos(a), -np.sin(a)], 0))
    w = np.concatenate([np.arange(1, W, 2), np.arange(0, W, 2)])
    a = turn * (ky[:, None] * w[None, :] % W)
    twice = np.where(ky == 0, 1.0, 2.0)[:, None] / NPIX
    f = np.concatenate([np.cos(a) * twice, -np.sin(a) * twice], 0)
    put("fi", np.concatenate([f, f], 0))
    put("ident", np.eye(P))
    k, m = np.arange(P)[:, None], np.arange(P)[None, :]
    same = (k % C) // GRP == (m % C) // GRP
    put("pair_re", same & (k < C))
    put("pair_all", same)
    put("diag2", (k % C == np.arange(C)[None, :]))
    put("diag_top", (k == np.arange(C)[None, :]))
    put("sgn", np.where(p < C, 1.0, -1.0))
    put("sgnh", np.where(p < C, 0.5, -0.5))
    return cst.astype(np.float32)


class Chain:

    def __init__(self, eng, sem, before, steps):
        self.eng, self.sem, self.before, self.steps, self.n = eng, sem, before, steps, 0

    def __call__(self, ins):
        self.n += 1
        ins.then_inc(self.sem, 1)
        self.eng.wait_ge(self.sem, self.before + self.n)

    def end(self):
        assert self.n == self.steps, self.n


def program(nc, x, w_pos_r, w_pos_i, w_neg_r, w_neg_i, ker, cst_in, out):
    modes_x = nc.dram_tensor("modes_x", [B, P, NKX * NKY], F32, kind="Internal").ap()
    modes_o = nc.dram_tensor("modes_o", [3, B, NKX, NKY * C], F32, kind="Internal").ap()

    with ExitStack() as ctx:
        sb = lambda name, shape, dt=F32: ctx.enter_context(nc.sbuf_tensor(name, shape, dt))
        sem = lambda name: ctx.enter_context(nc.semaphore(name))
        ps = ctx.enter_context(nc.psum_tensor("ps", [P, 8, 512], F32))
        cst = sb("cst", [P, NCONST])
        con = lambda name: cst[:, CW[name][0]:CW[name][1]]
        ident = con("ident")
        ones = sb("ones", [P, P])
        halves = sb("halves", [P, P])
        taps = sb("taps", [P, 4, 4, C])
        w_sq = sb("w_sq", [P, 1])
        mean0 = sb("mean0", [P, B])
        dev0 = sb("dev0", [P, B])
        fi_hi = sb("fi_hi", [P, W], F32R)
        fi_lo = sb("fi_lo", [P, W], F32R)
        setup(nc, cst_in, ker, ps, cst, con, ones, halves, taps, w_sq, fi_hi, fi_lo)
        phase_a(nc, x, modes_x, ps, con, cst_in[0:1, 0:8], ident, ones, mean0, dev0)
        phase_m(nc, (w_pos_r, w_pos_i), (w_neg_r, w_neg_i), modes_x, modes_o, ps, con, cst_in[0:1, 0:8], dev0)
        phase_b(nc, x, out, modes_x, modes_o, ps, con, cst_in[0:1, 0:8], ident, ones, halves, taps, w_sq, mean0, dev0, fi_hi, fi_lo)


def setup(nc, cst_in, ker, ps, cst, con, ones, halves, taps, w_sq, fi_hi, fi_lo):
    with ExitStack() as ctx:
        kw = ctx.enter_context(nc.sbuf_tensor("kw", [C, 9, 2, C], F32))
        w_part = ctx.enter_context(nc.sbuf_tensor("w_part", [P, 1], F32))
        w_junk = ctx.enter_context(nc.sbuf_tensor("w_junk", [P, 3 * 4 * C], F32))
        raw = ctx.enter_context(nc.sbuf_tensor("raw_taps", [P, 3, 4 * C], F32))
        sem = lambda name: ctx.enter_context(nc.semaphore(name))
        consts_in, kernels_in, filled, turned, squared, summed, split = map(
            sem, ("consts_in", "kernels_in", "filled", "turned", "w_squared", "w_summed", "fi_split"))
        block = ctx.enter_context(nc.Block())

        @block.sync
        def _(sync):
            sync.dma_start(cst[:, :], cst_in).then_inc(consts_in, 16)
            for r in range(2):
                sync.dma_start(kw[:, :, r, :], ker.rearrange("o y x i -> o (y x) i")).then_inc(kernels_in, 16)

        @block.tensor
        def _(pe):
            pe.wait_ge(consts_in, 16)
            pe.wait_ge(kernels_in, 32)
            ident64 = con("ident")[0:C, 0:C]
            for tap in range(9):
                last = nc.tensor.transpose(ps[:, tap // 8, (tap % 8) * C:(tap % 8 + 1) * C],
                                           kw[:, tap, :, :].rearrange("o r i -> o (r i)"), ident64)
            last.then_inc(turned, 1)
            pe.wait_ge(squared, 1)
            pe.wait_ge(filled, 2)
            nc.tensor.matmul(ps[:, 2, 0:1], halves[:, :], w_part[:, :], start=True, stop=True).then_inc(summed, 1)

        @block.vector
        def _(dve):
            nc.vector.memset(ones[:, :], 1.0).then_inc(filled, 1)
            nc.vector.memset(halves[:, :], 0.5).then_inc(filled, 1)
            nc.vector.memset(raw[:, :, :], 0.0).then_inc(filled, 1)
            dve.wait_ge(filled, 3)
            dve.wait_ge(turned, 1)
            for dx in range(3):
                for r in range(2):
                    for q in range(r, r + 3):
                        tap = (r + 2 - q) * 3 + dx
                        last = nc.vector.tensor_copy(raw[C * r:C * r + C, dx, C * q:C * q + C],
                                                     ps[C * r:C * r + C, tap // 8, (tap % 8) * C:(tap % 8 + 1) * C])
            last.then_inc(filled, 1)
            dve.wait_ge(filled, 4)
            flat = raw[:, :, :].rearrange("p a e -> p (a e)")
            nc.vector.scalar_tensor_tensor(w_junk[:, :], flat, 1.0, flat, ALU.mult, ALU.mult,
                                           accum_out=w_part[:, :]).then_inc(squared, 1)
            part = lambda i: taps[:, i, :, :].rearrange("p q o -> p (q o)")
            nc.vector.tensor_copy(part(0), raw[:, 0, :])
            nc.vector.tensor_copy(part(1), raw[:, 2, :]).then_inc(squared, 1)
            dve.wait_ge(squared, 2)
            nc.vector.tensor_tensor(raw[:, 0, :], raw[:, 0, :], raw[:, 2, :], ALU.add).then_inc(filled, 1)
            dve.wait_ge(filled, 5)
            nc.vector.tensor_scalar(raw[:, 0, :], raw[:, 0, :], 0.5, None, ALU.mult).then_inc(filled, 1)
            dve.wait_ge(filled, 6)
            nc.vector.scalar_tensor_tensor(part(2), raw[:, 1, :], 0.5, raw[:, 0, :], ALU.mult, ALU.add)
            nc.vector.scalar_tensor_tensor(part(3), raw[:, 1, :], 0.5, raw[:, 0, :], ALU.mult, ALU.subtract)
            dve.wait_ge(consts_in, 16)
            nc.vector.tensor_copy(fi_hi[:, :], con("fi")).then_inc(split, 1)
            dve.wait_ge(split, 1)
            nc.vector.tensor_tensor(fi_lo[:, :], con("fi"), fi_hi[:, :].bitcast(F32), ALU.subtract)
            dve.wait_ge(summed, 1)
            nc.vector.tensor_copy(w_sq[:, :], ps[:, 2, 0:1])


def phase_a(nc, x, modes_x, ps, con, con_in, ident, ones, mean0, dev0):
    NX = 8
    CB = 4
    CG = 16
    KB = 8
    NTR, NHG, NKB = C // CB, C // CG, NKY // KB
    x_v = x.rearrange("b (n r) (p j) c -> (b n) p r (j c)", r=RC, j=2)
    with ExitStack() as ctx:
        sb = lambda name, shape, dt=F32: ctx.enter_context(nc.sbuf_tensor(name, shape, dt))
        sem = lambda name: ctx.enter_context(nc.semaphore(name))
        xt = sb("a_xt", [P, NX, RC, 2 * C])
        sq = sb("a_sq", [P, 2, RC * 2 * C])
        acc = sb("a_acc", [P, RC * 2 * C])
        red = sb("a_red", [P, C // GRP])
        red4 = sb("a_red4", [P, 2, C // GRP, GRP])
        gw = sb("a_gw", [P, C, P])
        gh = sb("a_gh", [P, C, P])
        xh = sb("a_xh", [P, NKY, C])
        xc = sb("a_xc", [P, NKX, NKY])
        tmp = sb("a_tmp", [P, 8])
        seed = sb("a_seed", [1, 8])
        x_in = [sem(f"x_in{u}") for u in range(NX)]
        dft_done, dft_evac = sem("dft_done"), sem("dft_evac")
        sq_done, sq_used = sem("sq_done"), sem("sq_used")
        turned, gh_evac = sem("gw_turned"), sem("gh_evac")
        hdft_done, xh_evac = sem("hdft_done"), sem("xh_evac")
        mode_turned, xc_evac = sem("mode_turned"), sem("xc_evac")
        red_ready, sums_done, stats_step = sem("red_ready"), sem("sums_done"), sem("stats_step")
        xc_ready, xc_stored = sem("xc_ready"), sem("xc_stored")
        acc_summed, acc_cleared = sem("acc_summed"), sem("acc_cleared")
        block = ctx.enter_context(nc.Block())
        STATS = 6
        fw = con("fw").rearrange("p (j k) -> p j k", j=2)
        fh = con("fh").rearrange("p (g f k) -> p g f k", g=2, f=2)

        @block.sync
        def _(sync):
            def load(n, u):
                for half in (slice(0, RC // 2), slice(RC // 2, RC)):
                    sync.dma_start(xt[:, u, half, :], x_v[n][:, half]).then_inc(x_in[u], 16)

            for u in range(NX):
                load(u, u)
            with sync.Fori(0, NCH // NX - 1) as t:
                for u in range(NX):
                    sync.wait_ge(dft_done, t * NX + (u + 1))
                    sync.wait_ge(sq_done, t * NX + (u + 1))
                    load(t * NX + (u + NX), u)

        @block.tensor
        def _(pe):
            with pe.Fori(0, B) as b:
                with pe.Fori(0, CPI // NX) as t:
                    for u in range(NX):
                        pe.wait_ge(x_in[u], (b * (CPI // NX) + t) * 32 + 32)
                        pe.wait_ge(dft_evac, b * CPI + t * NX + (u + 1))
                        for j in range(2):
                            for g in range(2):
                                last = nc.tensor.matmul(ps[64 * g:64 * g + 64, u % 2, :], fw[:, j, :],
                                                        xt[:, u, 8 * g:8 * g + 8, C * j:C * j + C],
                                                        start=(j == 0), stop=(j == 1))
                        last.then_inc(dft_done, 1)
                pe.wait_ge(dft_evac, b * CPI + (CPI + 2))
                for q in range(NTR):
                    pe.wait_ge(gh_evac, b * NTR + (q + 1))
                    for i in range(CB):
                        last = nc.tensor.transpose(ps[:, 2 + q % 2, i * P:(i + 1) * P], gw[:, CB * q + i, :], ident)
                    last.then_inc(turned, 1)
                for q in range(NHG):
                    pe.wait_ge(gh_evac, b * NTR + ((q + 1) * CG // CB + 2))
                    pe.wait_ge(xh_evac, b * NHG + (q + 1))
                    for n, (g, f) in enumerate(((0, 0), (0, 1), (1, 0), (1, 1))):
                        lo = 64 * g + 32 * f
                        last = nc.tensor.matmul(ps[:, 4 + q % 2, :], fh[:, g, f, :],
                                                gh[:, CG * q:CG * (q + 1), lo:lo + NKY], start=(n == 0), stop=(n == 3))
                    last.then_inc(hdft_done, 1)
                pe.wait_ge(xh_evac, b * NHG + (NHG + 2))
                pe.wait_ge(red_ready, b + 1)
                for q in range(NKB):
                    pe.wait_ge(xc_evac, b * NKB + (q + 1))
                    for i in range(KB // 2):
                        ky = KB * q + 2 * i
                        last = nc.tensor.transpose(ps[:, 6 + q % 2, i * P:(i + 1) * P],
                                                   xh[:, ky:ky + 2, :].rearrange("p y c -> p (y c)"), ident)
                    last.then_inc(mode_turned, 1)
                pe.wait_ge(xc_evac, b * NKB + (NKB + 2))
                nc.tensor.matmul(ps[:, 6, 0:1], red4[:, :, :, :].rearrange("p a g e -> p (a g e)"),
                                 ones[:, 0:1], start=True, stop=True)
                nc.tensor.matmul(ps[:, 6, 1:2], con("pair_re"), xc[:, 0, 0:1],
                                 start=True, stop=True).then_inc(sums_done, 1)

        @block.scalar
        def _(act):
            with act.Fori(0, B) as b:
                with act.Fori(0, CPI // NX) as t:
                    for u in range(NX):
                        act.wait_ge(x_in[u], (b * (CPI // NX) + t) * 32 + 32)
                        act.wait_ge(sq_used, b * CPI + t * NX + (u + 1))
                        nc.scalar.activation(sq[:, u % 2, :], xt[:, u, :, :].rearrange("p r e -> p (r e)"),
                                             ACT.Square).then_inc(sq_done, 1)
                act.wait_ge(hdft_done, b * NHG + GIVEN)
                for q in range(NTR):
                    act.wait_ge(turned, b * NTR + (q + 1) + GIVEN)
                    nc.scalar.activation(gh[:, CB * q:CB * (q + 1), :].rearrange("p c k -> p (c k)"),
                                         ps[:, 2 + q % 2, :], ACT.Copy).then_inc(gh_evac, 1)
                act.wait_ge(xc_stored, b * 16 + 16)
                for q in range(NKB):
                    act.wait_ge(mode_turned, b * NKB + (q + 1) + GIVEN)
                    bank = ps[:, 6 + q % 2, :].rearrange("p (y f k) -> p f k y", y=KB // 2, f=2)
                    for f in range(2):
                        for e in range(2):
                            last = nc.scalar.activation(xc[C * f:C * f + C, :, KB * q + e:KB * (q + 1):2],
                                                        bank[C * e:C * e + C, f, :, :], ACT.Copy)
                    last.then_inc(xc_evac, 1)

        @block.vector
        def _(dve):
            nc.vector.memset(tmp[:, 0:1], 0.0).then_inc(dft_evac, 2)
            nc.vector.memset(tmp[:, 1:2], 0.0).then_inc(sq_used, 2)
            nc.vector.memset(tmp[:, 2:3], 0.0).then_inc(gh_evac, 2)
            nc.vector.memset(tmp[:, 3:4], 0.0).then_inc(xh_evac, 2)
            nc.vector.memset(red[:, :], 0.0).then_inc(xc_evac, 2)
            for i, s in enumerate((hdft_done, turned, sums_done, mode_turned)):
                nc.vector.memset(tmp[:, 4 + i:5 + i], 0.0).then_inc(s, GIVEN)
            nc.vector.memset(acc[:, :], 0.0).then_inc(acc_cleared, 1)
            with dve.Fori(0, B) as b:
                with dve.Fori(0, CPI // NX) as t:
                    for u in range(NX):
                        if u == 0:
                            dve.wait_ge(turned, b * NTR + GIVEN)
                            dve.wait_ge(acc_cleared, b + 1)
                        dve.wait_ge(dft_done, b * CPI + t * NX + (u + 1))
                        nc.vector.tensor_copy(gw[:, :, bass.ds(t * (8 * NX) + 8 * u, 8)],
                                              ps[:, u % 2, :].rearrange("p (r c) -> p c r", c=C)).then_inc(dft_evac, 1)
                        dve.wait_ge(sq_done, b * CPI + t * NX + (u + 1))
                        dve.wait_ge(sq_used, b * CPI + t * NX + (u + 2))
                        nc.vector.tensor_tensor(acc[:, :], acc[:, :], sq[:, u % 2, :], ALU.add).then_inc(sq_used, 1)
                dve.wait_ge(sq_used, b * CPI + (CPI + 2))
                dve.wait_ge(sums_done, b + GIVEN)
                nc.vector.tensor_reduce(red[:, :], acc[:, :].rearrange("p (m g e) -> p g m e", g=C // GRP, e=GRP),
                                        AX.XY, ALU.add).then_inc(acc_summed, 1)
                dve.wait_ge(acc_summed, b + 1)
                nc.vector.memset(acc[:, :], 0.0).then_inc(acc_cleared, 1)
                nc.vector.tensor_copy(red4[:, :, :, :],
                                      red[:, :].unsqueeze(1).unsqueeze(3).broadcast_to([P, 2, C // GRP, GRP]))\
                    .then_inc(red_ready, 1)
                dve.wait_ge(mode_turned, b * NKB + GIVEN)
                for q in range(NHG):
                    dve.wait_ge(hdft_done, b * NHG + (q + 1) + GIVEN)
                    nc.vector.tensor_copy(xh[:, :, CG * q:CG * (q + 1)],
                                          ps[:, 4 + q % 2, :].rearrange("p (c y) -> p y c", c=CG)).then_inc(xh_evac, 1)
                dve.wait_ge(sums_done, b + 1 + GIVEN)
                step = Chain(dve, stats_step, b * STATS, STATS)
                step(nc.vector.tensor_copy(tmp[:, 0:2], ps[:, 6, 0:2]))
                step(nc.vector.tensor_scalar(mean0[:, bass.ds(b, 1)], tmp[:, 1:2], 1.0 / NORM, None, ALU.mult))
                step(nc.vector.tensor_tensor(tmp[:, 2:3], tmp[:, 1:2], mean0[:, bass.ds(b, 1)], ALU.mult))
                step(nc.vector.tensor_tensor(dev0[:, bass.ds(b, 1)], tmp[:, 0:1], tmp[:, 2:3], ALU.subtract))
                step(nc.vector.tensor_scalar(tmp[:, 3:4], mean0[:, bass.ds(b, 1)], float(-NPIX), None, ALU.mult))
                step(nc.vector.tensor_tensor(xc[0:C, 0, 0:1], xc[0:C, 0, 0:1], tmp[0:C, 3:4], ALU.add))
                step.end()
                nc.vector.memset(tmp[:, 2:3], 0.0).then_inc(xc_ready, 1)

        @block.gpsimd
        def _(pool):
            pool.dma_start(seed[:, :], con_in).then_inc(xc_stored, 16)
            with pool.Fori(0, B) as b:
                pool.wait_ge(xc_ready, b + 1)
                pool.dma_start(modes_x[b], xc[:, :, :].rearrange("p k y -> p (k y)")).then_inc(xc_stored, 16)
            pool.wait_ge(xc_stored, B * 16 + 16)


def phase_m(nc, w_pos, w_neg, modes_x, modes_o, ps, con, con_in, dev0):
    KC = 4
    NM = NKX // KC
    MC = KC * NKY
    TQ = 4
    KT = NKY // TQ
    with ExitStack() as ctx:
        sb = lambda name, shape, dt=F32: ctx.enter_context(nc.sbuf_tensor(name, shape, dt))
        sem = lambda name: ctx.enter_context(nc.semaphore(name))
        wt = sb("m_w", [P, 2, C, MC])
        xs = sb("m_x", [P, 2, B, MC])
        st = sb("m_s", [P, 2, MC, 4 * B])
        ot = sb("m_o", [P, 2, KC, KT * C])
        seed = sb("m_seed", [1, 2, 8])
        rstd = sb("m_rstd", [P, 6, B])
        w_in = [sem(f"w_in{u}") for u in range(2)]
        xs_in = [sem(f"xs_in{u}") for u in range(2)]
        s_ready, o_done, o_evac, norm_step = sem("s_ready"), sem("o_done"), sem("o_evac"), sem("norm_step")
        var_ready, sqrt_done = sem("m_var_ready"), sem("m_sqrt_done")
        o_stored = [sem(f"o_stored{u}") for u in range(2)]
        block = ctx.enter_context(nc.Block())
        xs_v = modes_x.rearrange("b p (m e) -> m p b e", e=MC)
        w_v = [[w.rearrange("i o (m k) y -> m i o (k y)", k=KC) for w in pair] for pair in (w_pos, w_neg)]
        o_v = modes_o.rearrange("q b (m k) (t e) -> m t (q b) k e", k=KC, t=TQ)
        HALF = NM // 2

        @block.sync
        def _(sync):
            def load(sign, m_half, m, u):
                for ri in range(2):
                    sync.dma_start(wt[C * ri:C * ri + C, u, :, :], w_v[sign][ri][m_half]).then_inc(w_in[u], 16)
                sync.dma_start(xs[:, u, :, :], xs_v[m]).then_inc(xs_in[u], 16)

            for u in range(2):
                load(0, u, u, u)
            with sync.Fori(0, HALF // 2 - 1) as t:
                for u in range(2):
                    sync.wait_ge(o_done, t * (2 * KC) + (KC * (u + 1) + KC) + GIVEN)
                    load(0, t * 2 + (u + 2), t * 2 + (u + 2), u)
            with sync.Fori(0, HALF // 2) as t:
                for u in range(2):
                    sync.wait_ge(o_done, t * (2 * KC) + (KC * (HALF + u - 1) + KC) + GIVEN)
                    load(1, t * 2 + u, t * 2 + (HALF + u), u)

        @block.tensor
        def _(pe):
            with pe.Fori(0, NM // 2) as t:
                for u in range(2):
                    pe.wait_ge(w_in[u], t * 32 + 32)
                    pe.wait_ge(s_ready, t * 2 + (u + 1))
                    for k in range(KC):
                        pe.wait_ge(o_evac, t * (2 * KC) + (KC * u + k + 1))
                        for i in range(KT):
                            for tq in range(TQ):
                                mode = k * NKY + tq * KT + i
                                last = nc.tensor.matmul(ps[32 * tq:32 * tq + 32, KC * u + k, C * i:C * i + C],
                                                        st[:, u, mode, :], wt[:, u, :, mode], start=True, stop=True)
                        last.then_inc(o_done, 1)

        @block.vector
        def _(dve):
            nc.vector.memset(rstd[:, 5, 0:1], 0.0).then_inc(o_done, KC + GIVEN)
            nc.vector.memset(rstd[:, 5, 1:2], 0.0).then_inc(o_evac, 8)
            step = Chain(dve, norm_step, 0, 10)
            step(nc.vector.memset(st[:, :, :, 3 * B:], 0.0))
            step(nc.vector.tensor_scalar(rstd[:, 3, :], dev0[:, :], 1.0 / NORM, 0.0, ALU.mult, ALU.max))
            step(nc.vector.tensor_scalar(rstd[:, 3, :], rstd[:, 3, :], EPS, None, ALU.add))
            nc.vector.memset(rstd[:, 5, 0:1], 0.0).then_inc(var_ready, 1)
            dve.wait_ge(sqrt_done, 1)
            step(nc.vector.reciprocal(rstd[:, 0, :], rstd[:, 4, :]))
            step(nc.vector.tensor_tensor(rstd[:, 0, :], rstd[:, 0, :], rstd[:, 3, :], ALU.mult))
            step(nc.vector.tensor_tensor(rstd[:, 0, :], rstd[:, 0, :], rstd[:, 4, :], ALU.add))
            step(nc.vector.tensor_scalar(rstd[:, 5, :], rstd[:, 0, :], 0.5, None, ALU.mult))
            step(nc.vector.reciprocal(rstd[:, 0, :], rstd[:, 5, :]))
            step(nc.vector.tensor_scalar(rstd[:, 1, :], rstd[:, 0, :], con("sgn"), None, ALU.mult))
            step(nc.vector.tensor_scalar(rstd[:, 2, :], rstd[:, 1, :], -1.0, None, ALU.mult))
            step.end()
            with dve.Fori(0, NM // 2) as t:
                for u in range(2):
                    dve.wait_ge(xs_in[u], t * 16 + 16)
                    dve.wait_ge(o_done, t * (2 * KC) + KC * u + GIVEN)
                    cols = lambda q: st[:, u, :, q * B:(q + 1) * B].rearrange("p m b -> p b m")
                    scale = lambda row: rstd[:, row, :].unsqueeze(2).broadcast_to([P, B, MC])
                    nc.vector.tensor_tensor(cols(0), xs[:, u, :, :], scale(1), ALU.mult)
                    nc.vector.tensor_tensor(cols(2), xs[:, u, :, :], scale(2), ALU.mult)
                    nc.vector.tensor_tensor(cols(1)[C:P], xs[0:C, u, :, :], scale(0)[0:C], ALU.mult)
                    nc.vector.tensor_tensor(cols(1)[0:C], xs[C:P, u, :, :], scale(0)[C:P], ALU.mult).then_inc(s_ready, 1)

        @block.scalar
        def _(act):
            for u in range(2):
                act.dma_start(seed[:, u, :], con_in).then_inc(o_stored[u], 16)
            act.wait_ge(var_ready, 1)
            nc.scalar.activation(rstd[:, 4, :], rstd[:, 3, :], ACT.Sqrt).then_inc(sqrt_done, 1)
            with act.Fori(0, NM // 2) as t:
                for u in range(2):
                    act.wait_ge(o_stored[u], t * 64 + 16)
                    for k in range(KC):
                        act.wait_ge(o_done, t * (2 * KC) + (KC * u + k + 1 + KC) + GIVEN)
                        nc.scalar.activation(ot[:, u, k, :], ps[:, KC * u + k, :], ACT.Copy).then_inc(o_evac, 1)
                    act.wait_ge(o_evac, t * (2 * KC) + (KC * u + KC + 8))
                    for tq in range(TQ):
                        act.dma_start(o_v[t * 2 + u, tq], ot[32 * tq:32 * tq + 3 * B, u, :, :]).then_inc(o_stored[u], 16)
            for u in range(2):
                act.wait_ge(o_stored[u], NM // 2 * 64 + 16)


def phase_b(nc, x, out, modes_x, modes_o, ps, con, con_in, ident, ones, halves, taps, w_sq, mean0, dev0, fi_hi, fi_lo):
    RB = 8
    NB = H // RB
    BB = 4
    NIT = NB // BB
    OB = 2
    NY = H // 4
    RING = 16
    ZW = W + 2
    PH = P
    PARTS = (2, 3, 0, 1)
    NP = len(PARTS)
    NOT = NKY // 8
    NTB = C // 4
    Y0, CV = 0, 4
    x_v = x.rearrange("b (n r) (p j) c -> b n p j r c", r=RC, j=2)
    out_v = out.rearrange("b (n r) (p j) c -> b n p r (j c)", r=RB, j=2)
    with ExitStack() as ctx:
        sb = lambda name, shape, dt=F32: ctx.enter_context(nc.sbuf_tensor(name, shape, dt))
        sem = lambda name: ctx.enter_context(nc.semaphore(name))
        om = sb("b_om", [P, 2, NKY, C])
        xm = sb("b_xm", [P, NKX, NKY])
        oc = sb("b_oc", [P, NKX, NKY])
        sc = sb("b_sc", [P, 36])
        th = sb("b_th", [P, H, C], F32R)
        ts = sb("b_ts", [P, 4, RB, C], F32R)
        yb = sb("b_yb", [P, 4, 2, ZW])
        vb = sb("b_vb", [P, 4, 2, NP, PH])
        work = vb[:, 0:2, :, :, :].rearrange("p s k v e -> p (s k v e)")
        wf = vb[:, 2, :, :, :].rearrange("p k v e -> p (k v e)").rearrange("p (v q o) -> p v q o", v=NP, q=4)
        xt = sb("b_xt", [P, 2, 2, RC, C])
        zh = sb("b_zh", [P, RING, NP, PH], F16)
        zl = sb("b_zl", [P, RING, NP, PH], F16)
        wh = sb("b_wh", [P, NP, 4, C], F16)
        wl = sb("b_wl", [P, NP, 4, C], F16)
        ab = sb("b_ab", [P, RB * C])
        diag = sb("b_diag", [P, C])
        seed = sb("b_seed", [1, OB, 8])
        mrow = sb("b_mrow", [P, C])
        ob = sb("b_ob", [P, OB, RB, 2 * C])
        col = {n: sc[:, i:i + 1] for i, n in enumerate(
            ("a_rest", "a_ky0", "a_mirror", "a_dc", "part", "dc", "mean", "mean_d", "var", "sd", "sigma", "rstd",
             "w1", "w2", "fro", "froot", "f", "inv_f", "sigma_f", "neg_inv_f"))}
        om_in, xm_in = sem("om_in"), sem("xm_in")
        x_in = [sem(f"bx_in{u}") for u in range(2)]
        oc_turned, oc_even, oc_odd = sem("oc_turned"), sem("oc_even"), sem("oc_odd")
        part_ready, group_done, var_ready, sd_ready = map(sem, ("part_ready", "group_done", "b_var_ready", "sd_ready"))
        sig_done, fro_ready, froot_ready = map(sem, ("sig_done", "fro_ready", "froot_ready"))
        w_ready, mean_ready, mrow_done, om_fixed = map(sem, ("w_ready", "mean_ready", "mrow_done", "om_fixed"))
        t_done, t_hi, t_lo, ts_ready = map(sem, ("t_done", "t_hi", "t_lo", "ts_ready"))
        y_done, y_evac, v_sum, v_diff = map(sem, ("y_done", "y_evac", "v_sum", "v_diff"))
        z_hi, z_lo, conv_done, out_evac = map(sem, ("z_hi", "z_lo", "conv_done", "out_evac"))
        out_stored = [sem(f"out_stored{u}") for u in range(OB)]
        bstep, cleared = sem("bstep"), sem("cleared")
        block = ctx.enter_context(nc.Block())
        YG = 8
        SLOT = 4
        STEPS = 36

        @block.sync
        def _(sync):
            def load_x(b, n, u):
                for j in range(2):
                    sync.dma_start(xt[:, u, j, :, :], x_v[b, n][:, j]).then_inc(x_in[u], 16)

            def body(b, it, last=False):
                for kk in range(BB):
                    if kk % 2 == 0 and not last:
                        sync.wait_ge(y_done, b * NY + it * (2 * BB) + (2 * kk + 4 + YG))
                        load_x(b, it * 2 + (kk // 2 + 2), kk // 2)
                    sync.wait_ge(out_evac, b * (NP * NB) + it * (NP * BB) + NP * (kk + 1) + NP)
                    sync.dma_start(out_v[b, it * BB + kk], ob[:, kk % OB, :, :]).then_inc(out_stored[kk % OB], 16)

            for u in range(OB):
                sync.dma_start(seed[:, u, :], con_in).then_inc(out_stored[u], 16)
            with sync.Fori(0, B) as b:
                sync.wait_ge(t_done, b * NTB + GIVEN)
                for form in range(2):
                    for ri in range(2):
                        sync.dma_start(om[NKX * ri:NKX * ri + NKX, form, :, :].rearrange("p y o -> p (y o)"),
                                       modes_o[form + ri, b]).then_inc(om_in, 16)
                sync.wait_ge(part_ready, b + GIVEN)
                sync.dma_start(xm[:, :, :].rearrange("p k y -> p (k y)"), modes_x[b]).then_inc(xm_in, 16)
                sync.wait_ge(y_done, b * NY + YG)
                for u in range(2):
                    load_x(b, u, u)
                with sync.Fori(0, NIT - 1) as it:
                    body(b, it)
                body(b, NIT - 1, last=True)
            for u in range(OB):
                sync.wait_ge(out_stored[u], B * (NB // OB) * 16 + 16)

        @block.tensor
        def _(pe):
            def y_bank(b, it, n):
                u = (n // 4) % 2
                if n % 4 == 0:
                    uses = b * (CPI // 2) + it + (n // 8)
                    pe.wait_ge(x_in[u], uses * 32 + 32)
                pe.wait_ge(ts_ready, b * NB + it * BB + (n // 2 + 1) + GIVEN)
                if isinstance(it, int) and 2 * BB * it + n < 4:
                    pe.wait_ge(t_lo, b * NTB + NTB)
                else:
                    pe.wait_ge(y_evac, b * NY + it * (2 * BB) + (n - 3) + GIVEN)
                bank = Y0 + n % 4
                for k in range(2):
                    r = (n % 4) * 4 + 2 * k
                    for jj in range(2):
                        j = 1 - jj
                        nc.tensor.matmul(ps[:, bank, k * W + jj * P:k * W + (jj + 1) * P],
                                         xt[:, u, j, r:r + 2, :].rearrange("p r c -> p (r c)"), ident, is_transpose=True,
                                         start=(k == 0 and jj == 0), stop=False, skip_group_check=True)
                for k in range(2):
                    r = (n % 4) * 4 + 2 * k
                    for f in (fi_hi, fi_lo):
                        last = nc.tensor.matmul(ps[:, bank, k * W:(k + 1) * W],
                                                ts[:, (n // 2) % 4, r % RB:r % RB + 2, :].rearrange("p r c -> p (r c)"), f[:, :],
                                                start=False, stop=(f is fi_lo and k == 1), skip_group_check=True)
                last.then_inc(y_done, 1)

            def conv_block(b, it, kk, first, last_block):
                done = b * (NP * NB) + it * (NP * BB) + NP * kk
                pe.wait_ge(z_lo, b * NY + it * (2 * BB) + (2 * kk + (2 if last_block else 3)) + SLOT)
                if first:
                    pe.wait_ge(w_ready, b + 1 + GIVEN)
                pairs = range(4 * kk - (0 if first else 1), 4 * kk + (4 if last_block else 5))
                pairs = sorted(pairs, key=lambda q: not 4 * kk <= q < 4 * kk + 4)
                for i, part in enumerate(PARTS):
                    pe.wait_ge(out_evac, done + i + 1)
                    n, total = 0, 3 * len(pairs)
                    for z, w in ((zh, wh), (zl, wh), (zh, wl)):
                        for pair in pairs:
                            row = 2 * pair - 1 - RB * kk
                            q0, q1 = max(0, -row), min(4, RB - row)
                            last = nc.tensor.matmul(
                                ps[:, CV + i, (row + q0) * C:(row + q1) * C],
                                z[:, pair % RING, part, :],
                                w[:, part, q0:q1, :].rearrange("p q o -> p (q o)"),
                                start=(n == 0), stop=(n == total - 1), skip_group_check=True)
                            n += 1
                    last.then_inc(conv_done, 1)

            def body(b, it, first=False, last=False):
                for kk in range(BB):
                    for n in (2 * kk + 3, 2 * kk + 4):
                        if not (last and n >= 2 * BB):
                            y_bank(b, it, n)
                    conv_block(b, it, kk, first and kk == 0, last and kk == BB - 1)

            with pe.Fori(0, B) as b:
                pe.wait_ge(om_in, b * 64 + 64)
                pe.wait_ge(y_evac, b * NY + GIVEN)
                for q in range(NOT):
                    for i in range(4):
                        ky = 8 * q + 2 * i
                        last = nc.tensor.transpose(ps[:, Y0 + q, i * P:(i + 1) * P],
                                                   om[:, 0, ky:ky + 2, :].rearrange("p y c -> p (y c)"), ident)
                    last.then_inc(oc_turned, 1)
                pe.wait_ge(out_evac, b * (NP * NB) + NP)
                pe.wait_ge(part_ready, b + 1 + GIVEN)
                nc.tensor.matmul(ps[:, CV, 0:1], con("pair_all"), col["part"], start=True, stop=True)
                nc.tensor.matmul(ps[:, CV, 1:2], con("pair_re"), col["dc"], start=True, stop=True).then_inc(group_done, 1)
                pe.wait_ge(var_ready, b + 1)
                nc.tensor.matmul(ps[:, CV + 1, 0:1], halves[:, :], col["var"], start=True, stop=True).then_inc(sig_done, 1)
                pe.wait_ge(mean_ready, b + 1)
                nc.tensor.matmul(ps[:, CV + 2, 0:C], ones[:, :], diag[:, :], start=True, stop=True).then_inc(mrow_done, 1)
                pe.wait_ge(om_fixed, b + 1)
                for q in range(NTB):
                    if q < 4:
                        pe.wait_ge(oc_even, b * NOT + (q + 1))
                        pe.wait_ge(oc_odd, b * NOT + (q + 1))
                    else:
                        pe.wait_ge(t_lo, b * NTB + (q - 3))
                    for i in range(2):
                        for half in range(2):
                            c = 2 * q + i + half * (C // 2)
                            last = nc.tensor.matmul(ps[64 * half:64 * half + 64, Y0 + q % 4, i * H:(i + 1) * H],
                                                    om[:, :, :, c].rearrange("p f y -> p (f y)"), con("eh"),
                                                    start=True, stop=True)
                    last.then_inc(t_done, 1)
                for n in range(3):
                    y_bank(b, 0, n)
                body(b, 0, first=True)
                with pe.Fori(1, NIT - 1) as it:
                    body(b, it)
                body(b, NIT - 1, last=True)

        def z_slot(t, n):
            return t[:, (2 * n) % RING:(2 * n) % RING + 2, :, :].rearrange("p k v e -> p (k v e)")

        def v_slot(n):
            return vb[:, n % 4, :, :, :].rearrange("p k v e -> p (k v e)")

        def y_order(nit_last):
            return [[n for n in (2 * kk + 3, 2 * kk + 4) if not (nit_last and n >= 2 * BB)] for kk in range(BB)]

        @block.scalar
        def _(act):
            def rows(b, it, m):
                act.wait_ge(y_done, b * NY + it * (2 * BB) + (2 * m + 2))
                nc.scalar.activation(ts[:, m % 4, :, :], th[:, bass.ds(it * (BB * RB) + m * RB, RB), :].bitcast(F32), ACT.Copy)\
                    .then_inc(ts_ready, 1)

            def take_y(b, it, n):
                act.wait_ge(y_done, b * NY + it * (2 * BB) + (n + 1 + YG))
                for s in (v_sum, v_diff):
                    act.wait_ge(s, b * NY + it * (2 * BB) + (n + 1))
                nc.scalar.activation(yb[:, n % 4, :, 1:1 + W], ps[:, Y0 + n % 4, :].rearrange("p (k w) -> p k w", k=2),
                                     ACT.Copy, scale=col["rstd"]).then_inc(y_evac, 1)

            def high(b, it, n, blocks):
                for s in (v_sum, v_diff):
                    act.wait_ge(s, b * NY + it * (2 * BB) + (n + 1 + SLOT))
                act.wait_ge(conv_done, blocks * NP + GIVEN)
                nc.scalar.activation(z_slot(zh, n), v_slot(n), ACT.Copy).then_inc(z_hi, 1)

            def body(b, it, first=False, last=False):
                for kk, banks in enumerate(y_order(last)):
                    if not (last and kk + 3 >= BB):
                        rows(b, it, kk + 3)
                    for n in banks:
                        take_y(b, it, n)
                    for n in banks:
                        high(b, it, n, b * NB if first and kk == 0 else b * NB + it * BB + (kk - 1))

            with act.Fori(0, B) as b:
                act.wait_ge(w_ready, b + GIVEN)
                for q in range(NOT):
                    act.wait_ge(oc_turned, b * NOT + (q + 1))
                    bank = ps[:, Y0 + q, :].rearrange("p (y f k) -> p f k y", y=4, f=2)
                    for f in range(2):
                        last = nc.scalar.activation(oc[C * f:C * f + C, :, 8 * q:8 * q + 8:2], bank[0:C, f, :, :], ACT.Copy)
                    last.then_inc(oc_even, 1)
                act.wait_ge(var_ready, b + 1)
                nc.scalar.activation(col["sd"], col["var"], ACT.Sqrt).then_inc(sd_ready, 1)
                act.wait_ge(fro_ready, b + 1)
                nc.scalar.activation(col["froot"], col["fro"], ACT.Sqrt).then_inc(froot_ready, 1)
                act.wait_ge(ts_ready, b * NB + GIVEN)
                for q in range(NTB):
                    act.wait_ge(t_done, b * NTB + (q + 1) + GIVEN)
                    for half in range(2):
                        c = 2 * q + half * (C // 2)
                        last = nc.scalar.activation(
                            th[64 * half:64 * half + 64, :, c:c + 2],
                            ps[64 * half:64 * half + 64, Y0 + q % 4, :].rearrange("p (c h) -> p h c", c=2), ACT.Copy)
                    last.then_inc(t_hi, 1)
                act.wait_ge(w_ready, b + 1 + GIVEN)
                act.wait_ge(cleared, 1)
                act.wait_ge(t_lo, b * NTB + NTB)
                for m in range(3):
                    rows(b, 0, m)
                for n in range(3):
                    take_y(b, 0, n)
                for n in range(3):
                    high(b, 0, n, b * NB)
                body(b, 0, first=True)
                with act.Fori(1, NIT - 1) as it:
                    body(b, it)
                body(b, NIT - 1, last=True)

        @block.vector
        def _(dve):
            v = nc.vector

            def sums(b, it, n):
                dve.wait_ge(y_evac, b * NY + it * (2 * BB) + (n + 1 + GIVEN))
                dve.wait_ge(z_lo, b * NY + it * (2 * BB) + (n + 1))
                even, odd = yb[:, n % 4, :, 1 + PH:1 + W], yb[:, n % 4, :, 1:1 + PH]
                v.tensor_tensor(vb[:, n % 4, :, 2, :], even, odd, ALU.add)
                v.tensor_tensor(vb[:, n % 4, :, 3, :], even, odd, ALU.subtract).then_inc(v_sum, 1)

            def low(b, it, n):
                dve.wait_ge(z_hi, b * NY + it * (2 * BB) + (n + 1))
                v.tensor_tensor(z_slot(zl, n), v_slot(n), z_slot(zh, n), ALU.subtract).then_inc(z_lo, 1)

            def take(b, it, kk, i):
                done = b * (NP * NB) + it * (NP * BB) + NP * kk
                dve.wait_ge(conv_done, done + (i + 1) + GIVEN)
                bank = ps[:, CV + i, :].rearrange("p (r o) -> p r o", o=C)
                m1 = ab[:, :].rearrange("p (r o) -> p r o", o=C)
                even, odd = ob[:, kk % OB, :, 0:C], ob[:, kk % OB, :, C:2 * C]
                if i == 0:
                    v.scalar_tensor_tensor(m1, bank, col["inv_f"], mrow[:, :].unsqueeze(1).broadcast_to([P, RB, C]),
                                           ALU.mult, ALU.add).then_inc(out_evac, 1)
                elif i == 1:
                    dve.wait_ge(out_stored[kk % OB], (b * (NB // OB) + it * (BB // OB) + kk // OB) * 16 + 16)
                    dve.wait_ge(out_evac, done + NP + 1)
                    v.scalar_tensor_tensor(even, bank, col["inv_f"], m1, ALU.mult, ALU.add)
                    v.scalar_tensor_tensor(odd, bank, col["neg_inv_f"], m1, ALU.mult, ALU.add).then_inc(out_evac, 1)
                else:
                    dve.wait_ge(out_evac, done + NP + 2)
                    side, scale = ((even, col["inv_f"]), (odd, col["neg_inv_f"]))[i - 2]
                    v.scalar_tensor_tensor(side, bank, scale, side, ALU.mult, ALU.add).then_inc(out_evac, 1)

            def body(b, it, first=False, last=False):
                for kk, banks in enumerate(y_order(last)):
                    if not (first and kk == 0):
                        take(b, it - 1 if kk == 0 else it, (kk - 1) % BB, 3)
                    for n in banks:
                        sums(b, it, n)
                    take(b, it, kk, 0)
                    for n in banks[:1]:
                        low(b, it, n)
                    take(b, it, kk, 1)
                    for n in banks[1:]:
                        low(b, it, n)
                    take(b, it, kk, 2)

            v.memset(sc[:, 23:24], 0.0).then_inc(y_done, YG)
            for i, (s, given) in enumerate(((t_done, GIVEN), (part_ready, GIVEN), (w_ready, GIVEN), (ts_ready, GIVEN),
                                            (conv_done, GIVEN), (y_evac, GIVEN), (out_evac, NP),
                                            (z_lo, SLOT), (v_sum, SLOT), (v_diff, SLOT))):
                v.memset(sc[:, 24 + i:25 + i], 0.0).then_inc(s, given)
            v.memset(yb[:, :, :, 0:1], 0.0)
            v.memset(yb[:, :, :, 1 + W:], 0.0).then_inc(cleared, 1)
            with dve.Fori(0, B) as b:
                for q in range(NOT):
                    dve.wait_ge(oc_turned, b * NOT + (q + 1))
                    bank = ps[:, Y0 + q, :].rearrange("p (y f k) -> p f k y", y=4, f=2)
                    for f in range(2):
                        last = v.tensor_copy(oc[C * f:C * f + C, :, 8 * q + 1:8 * q + 8:2], bank[C:P, f, :, :])
                    last.then_inc(oc_odd, 1)
                dve.wait_ge(oc_even, b * NOT + NOT)
                dve.wait_ge(oc_odd, b * NOT + NOT)
                dve.wait_ge(xm_in, b * 16 + 16)
                step = Chain(dve, bstep, b * STEPS, STEPS)
                rest = work[:, 0:NKX * (NKY - 1)].rearrange("p (k y) -> p k y", k=NKX)
                ky0 = work[:, 0:NKX]
                step(v.scalar_tensor_tensor(rest, xm[:, :, 1:], 2.0, oc[:, :, 1:], ALU.mult, ALU.add))
                step(v.scalar_tensor_tensor(rest, rest, 1.0, oc[:, :, 1:], ALU.mult, ALU.mult, accum_out=col["a_rest"]))
                step(v.scalar_tensor_tensor(ky0, xm[:, :, 0], 4.0, oc[:, :, 0], ALU.mult, ALU.add))
                step(v.scalar_tensor_tensor(ky0, ky0, 1.0, oc[:, :, 0], ALU.mult, ALU.mult, accum_out=col["a_ky0"]))
                step(v.scalar_tensor_tensor(work[:, 0:31], oc[:, 1:32, 0], 2.0, oc[:, 63:32:-1, 0],
                                            ALU.mult, ALU.mult, accum_out=col["a_mirror"]))
                step(v.tensor_tensor(col["a_dc"], oc[:, 0, 0:1], oc[:, 0, 0:1], ALU.mult))
                step(v.tensor_tensor(col["w1"], col["a_mirror"], col["a_dc"], ALU.add))
                step(v.tensor_tensor(col["w1"], col["w1"], con("sgnh"), ALU.mult))
                step(v.scalar_tensor_tensor(col["w2"], col["a_ky0"], 0.5, col["w1"], ALU.mult, ALU.add))
                step(v.scalar_tensor_tensor(col["part"], col["a_rest"], 2.0, col["w2"], ALU.mult, ALU.add))
                step(v.tensor_tensor(col["dc"], oc[:, 0, 0:1], xm[:, 0, 0:1], ALU.add))
                v.memset(sc[:, 23:24], 0.0).then_inc(part_ready, 1)
                dve.wait_ge(group_done, b + 1)
                step(v.tensor_scalar(col["mean_d"], ps[:, CV, 1:2], 1.0 / NORM, None, ALU.mult))
                step(v.tensor_tensor(col["mean"], col["mean_d"], mean0[:, bass.ds(b, 1)], ALU.add))
                step(v.scalar_tensor_tensor(col["w1"], ps[:, CV, 0:1], 1.0 / NPIX, dev0[:, bass.ds(b, 1)], ALU.mult, ALU.add))
                step(v.tensor_tensor(col["w2"], col["mean_d"], col["mean_d"], ALU.mult))
                step(v.scalar_tensor_tensor(col["w1"], col["w1"], 1.0 / NORM, col["w2"], ALU.mult, ALU.subtract))
                step(v.tensor_scalar(col["var"], col["w1"], 0.0, EPS, ALU.max, ALU.add))
                v.tensor_scalar(diag[:, :], con("diag_top"), col["mean"], None, ALU.mult).then_inc(mean_ready, 1)
                v.memset(sc[:, 23:24], 0.0).then_inc(var_ready, 1)
                dve.wait_ge(mrow_done, b + 1)
                step(v.tensor_copy(mrow[:, :], ps[:, CV + 2, 0:C]))
                step(v.scalar_tensor_tensor(om[0:1, 0, 0, :], mrow[0:1, :], float(-NPIX), om[0:1, 0, 0, :], ALU.mult, ALU.add))
                step(v.scalar_tensor_tensor(om[NKX:NKX + 1, 1, 0, :], mrow[NKX:NKX + 1, :], float(NPIX),
                                            om[NKX:NKX + 1, 1, 0, :], ALU.mult, ALU.add))
                v.memset(sc[:, 23:24], 0.0).then_inc(om_fixed, 1)
                dve.wait_ge(sig_done, b + 1)
                step(v.tensor_tensor(col["fro"], ps[:, CV + 1, 0:1], w_sq[:, :], ALU.add))
                v.memset(sc[:, 23:24], 0.0).then_inc(fro_ready, 1)
                dve.wait_ge(sd_ready, b + 1)
                step(v.reciprocal(col["w1"], col["sd"]))
                step(v.tensor_tensor(col["w1"], col["w1"], col["var"], ALU.mult))
                step(v.tensor_tensor(col["w1"], col["w1"], col["sd"], ALU.add))
                step(v.tensor_scalar(col["sigma"], col["w1"], 0.5, None, ALU.mult))
                step(v.reciprocal(col["rstd"], col["sigma"]))
                dve.wait_ge(froot_ready, b + 1)
                step(v.reciprocal(col["w2"], col["froot"]))
                step(v.tensor_scalar(col["f"], col["w2"], WSCALE, None, ALU.mult))
                step(v.reciprocal(col["inv_f"], col["f"]))
                step(v.tensor_scalar(col["neg_inv_f"], col["inv_f"], -1.0, None, ALU.mult))
                step(v.scalar_tensor_tensor(col["sigma_f"], col["sigma"], 0.5, col["f"], ALU.mult, ALU.mult))
                step(v.tensor_scalar(wf.rearrange("p a q o -> p (a q o)"),
                                     taps[:, :, :, :].rearrange("p a q o -> p (a q o)"), col["f"], None, ALU.mult))
                for r in range(2):
                    half = slice(C * r, C * r + C)
                    step(v.scalar_tensor_tensor(wf[half, 2:4, 1 + r, :],
                                                con("diag2")[half].unsqueeze(1).broadcast_to([C, 2, C]), col["sigma_f"][half],
                                                wf[half, 2:4, 1 + r, :], ALU.mult, ALU.add))
                dve.wait_ge(conv_done, b * (NP * NB) + GIVEN)
                step(v.tensor_copy(wh[:, :, :, :].rearrange("p a q o -> p (a q o)"),
                                   wf.rearrange("p a q o -> p (a q o)")))
                step(v.tensor_tensor(wl[:, :, :, :], wf[:, :, :, :], wh[:, :, :, :], ALU.subtract))
                step.end()
                v.memset(sc[:, 23:24], 0.0).then_inc(w_ready, 1)
                for q in range(NTB):
                    dve.wait_ge(t_hi, b * NTB + (q + 1))
                    for half in range(2):
                        c = 2 * q + half * (C // 2)
                        mine, other = slice(64 * half, 64 * half + 64), slice(64 * (1 - half), 64 * (1 - half) + 64)
                        last = v.tensor_tensor(th[other, :, c:c + 2],
                                               ps[mine, Y0 + q % 4, :].rearrange("p (c h) -> p h c", c=2),
                                               th[mine, :, c:c + 2].bitcast(F32), ALU.subtract)
                    last.then_inc(t_lo, 1)
                for n in range(3):
                    sums(b, 0, n)
                for n in range(3):
                    low(b, 0, n)
                body(b, 0, first=True)
                with dve.Fori(1, NIT - 1) as it:
                    body(b, it)
                body(b, NIT - 1, last=True)
                take(b, NIT - 1, BB - 1, 3)

        @block.gpsimd
        def _(pool):
            def diffs(b, it, n):
                pool.wait_ge(y_evac, b * NY + it * (2 * BB) + (n + 1 + GIVEN))
                pool.wait_ge(z_lo, b * NY + it * (2 * BB) + (n + 1))
                cols = yb[:, n % 4, :, :].rearrange("p k (g e) -> p k g e", g=2)
                nc.gpsimd.tensor_tensor(vb[:, n % 4, :, 0:2, :], cols[:, :, :, 0:PH], cols[:, :, :, 1:1 + PH], ALU.subtract)\
                    .then_inc(v_diff, 1)

            with pool.Fori(0, B) as b:
                for n in range(3):
                    diffs(b, 0, n)
                with pool.Fori(0, NIT - 1) as it:
                    for n in range(3, 3 + 2 * BB):
                        diffs(b, it, n)
                for n in range(3, 2 * BB):
                    diffs(b, NIT - 1, n)


_INS = ["x", "L0_conv_w_pos_r", "L0_conv_w_pos_i", "L0_conv_w_neg_r", "L0_conv_w_neg_i", "L1_conv_kernels"]


def kernel(**inputs):
    import concourse.bacc as bacc
    from concourse.bass_utils import run_bass_kernel_spmd

    nc = bacc.Bacc("TRN2", target_bir_lowering=False, num_devices=1)
    arrays, args = {}, []
    for name in _INS:
        arrays[name] = np.ascontiguousarray(inputs[name])
    arrays["constants"] = constants()
    for name, a in arrays.items():
        args.append(nc.dram_tensor(name, a.shape, mybir.dt.from_np(a.dtype), kind="ExternalInput").ap())
    out = nc.dram_tensor("out", (B, H, W, C), F32, kind="ExternalOutput").ap()
    program(nc, *args, out)
    r = run_bass_kernel_spmd(nc, [arrays], core_ids=[0])
    return r.results[0]["out"]
```

```python
import numpy as np
import concourse.bass as bass
from concourse import mybir
from contextlib import ExitStack

F32 = mybir.dt.float32
F32R = mybir.dt.float32r
F16 = mybir.dt.float16
ALU = mybir.AluOpType
ACT = mybir.ActivationFunctionType
AX = mybir.AxisListType

P = 128
B, H, W, C = 8, 256, 256, 64
NKX, NKY = 64, 32
NPIX = H * W
GRP = 2
NORM = float(GRP * NPIX)
EPS = 1e-5
RC = 16
CPI = H // RC
NCH = B * CPI
GIVEN = 1
KC = 4
MC = KC * NKY
WSCALE = 8192.0

CW = {}
_at = 0
for _name, _n in (("fw", 2 * 64), ("fh", 4 * 128), ("eh", 256), ("fi", 256), ("ident", 128),
                  ("pair_re", 128), ("pair_all", 128), ("diag2", 64), ("diag_top", 64), ("sgn", 1), ("sgnh", 1)):
    CW[_name] = (_at, _at + _n)
    _at += _n
NCONST = _at


def constants():
    cst = np.zeros((P, NCONST), np.float64)

    def put(name, a):
        cst[:, CW[name][0]:CW[name][1]] = np.asarray(a).reshape(P, -1)

    turn = 2 * np.pi / W
    p, ky, j = np.arange(P), np.arange(NKY), np.arange(2)
    a = turn * ((2 * p[:, None, None] + j[None, :, None]) * ky[None, None, :] % W)
    put("fw", np.concatenate([np.cos(a), -np.sin(a)], -1))
    kx = np.arange(NKX)
    kx = np.where(kx < NKX // 2, kx, kx - NKX)
    h = (p[:, None] // 8) * 16 + p[:, None] % 8 + 8 * np.arange(2)[None, :]
    a = turn * (h[:, :, None] * kx[None, None, :] % H)
    re = np.concatenate([np.cos(a), -np.sin(a)], -1)
    im = np.concatenate([np.sin(a), np.cos(a)], -1)
    put("fh", np.stack([re, im], 2))
    a = turn * (kx[:, None] * np.arange(H)[None, :] % H)
    put("eh", np.concatenate([np.cos(a), -np.sin(a)], 0))
    w = np.concatenate([np.arange(1, W, 2), np.arange(0, W, 2)])
    a = turn * (ky[:, None] * w[None, :] % W)
    twice = np.where(ky == 0, 1.0, 2.0)[:, None] / NPIX
    f = np.concatenate([np.cos(a) * twice, -np.sin(a) * twice], 0)
    put("fi", np.concatenate([f, f], 0))
    put("ident", np.eye(P))
    k, m = np.arange(P)[:, None], np.arange(P)[None, :]
    same = (k % C) // GRP == (m % C) // GRP
    put("pair_re", same & (k < C))
    put("pair_all", same)
    put("diag2", (k % C == np.arange(C)[None, :]))
    put("diag_top", (k == np.arange(C)[None, :]))
    put("sgn", np.where(p < C, 1.0, -1.0))
    put("sgnh", np.where(p < C, 0.5, -0.5))
    return cst.astype(np.float32)


class Chain:

    def __init__(self, eng, sem, before, steps):
        self.eng, self.sem, self.before, self.steps, self.n = eng, sem, before, steps, 0

    def __call__(self, ins):
        self.n += 1
        ins.then_inc(self.sem, 1)
        self.eng.wait_ge(self.sem, self.before + self.n)

    def end(self):
        assert self.n == self.steps, self.n


def program(nc, x, w_pos_r, w_pos_i, w_neg_r, w_neg_i, ker, cst_in, out):
    modes_x = nc.dram_tensor("modes_x", [B, P, NKX * NKY], F32, kind="Internal").ap()
    modes_o = nc.dram_tensor("modes_o", [3, B, NKX, NKY * C], F32, kind="Internal").ap()

    with ExitStack() as ctx:
        sb = lambda name, shape, dt=F32: ctx.enter_context(nc.sbuf_tensor(name, shape, dt))
        sem = lambda name: ctx.enter_context(nc.semaphore(name))
        ps = ctx.enter_context(nc.psum_tensor("ps", [P, 8, 512], F32))
        cst = sb("cst", [P, NCONST])
        con = lambda name: cst[:, CW[name][0]:CW[name][1]]
        ident = con("ident")
        ones = sb("ones", [P, P])
        halves = sb("halves", [P, P])
        taps = sb("taps", [P, 4, 4, C])
        w_sq = sb("w_sq", [P, 1])
        mean0 = sb("mean0", [P, B])
        dev0 = sb("dev0", [P, B])
        fi_hi = sb("fi_hi", [P, W], F32R)
        fi_lo = sb("fi_lo", [P, W], F32R)
        setup(nc, cst_in, ker, ps, cst, con, ones, halves, taps, w_sq, fi_hi, fi_lo)
        with ExitStack() as ctx_am:
            room = ctx_am.enter_context(nc.sbuf_tensor("room", [P, 2 * C * MC], F32))
            w_first = [ctx_am.enter_context(nc.semaphore(f"w_in{u}")) for u in range(2)]
            phase_a(nc, x, (w_pos_r, w_pos_i), modes_x, ps, con, cst_in[0:1, 0:8], ident, ones, mean0, dev0, room, w_first)
            phase_m(nc, (w_pos_r, w_pos_i), (w_neg_r, w_neg_i), modes_x, modes_o, ps, con, cst_in[0:1, 0:8], dev0, room, w_first)
        phase_b(nc, x, out, modes_x, modes_o, ps, con, cst_in[0:1, 0:8], ident, ones, halves, taps, w_sq, mean0, dev0, fi_hi, fi_lo)


def setup(nc, cst_in, ker, ps, cst, con, ones, halves, taps, w_sq, fi_hi, fi_lo):
    with ExitStack() as ctx:
        kw = ctx.enter_context(nc.sbuf_tensor("kw", [C, 9, 2, C], F32))
        w_part = ctx.enter_context(nc.sbuf_tensor("w_part", [P, 1], F32))
        w_junk = ctx.enter_context(nc.sbuf_tensor("w_junk", [P, 3 * 4 * C], F32))
        raw = ctx.enter_context(nc.sbuf_tensor("raw_taps", [P, 3, 4 * C], F32))
        sem = lambda name: ctx.enter_context(nc.semaphore(name))
        consts_in, kernels_in, filled, turned, squared, summed, split = map(
            sem, ("consts_in", "kernels_in", "filled", "turned", "w_squared", "w_summed", "fi_split"))
        block = ctx.enter_context(nc.Block())

        @block.sync
        def _(sync):
            sync.dma_start(cst[:, :], cst_in).then_inc(consts_in, 16)
            for r in range(2):
                sync.dma_start(kw[:, :, r, :], ker.rearrange("o y x i -> o (y x) i")).then_inc(kernels_in, 16)

        @block.tensor
        def _(pe):
            pe.wait_ge(consts_in, 16)
            pe.wait_ge(kernels_in, 32)
            ident64 = con("ident")[0:C, 0:C]
            for tap in range(9):
                last = nc.tensor.transpose(ps[:, tap // 8, (tap % 8) * C:(tap % 8 + 1) * C],
                                           kw[:, tap, :, :].rearrange("o r i -> o (r i)"), ident64)
            last.then_inc(turned, 1)
            pe.wait_ge(squared, 1)
            pe.wait_ge(filled, 2)
            nc.tensor.matmul(ps[:, 2, 0:1], halves[:, :], w_part[:, :], start=True, stop=True).then_inc(summed, 1)

        @block.vector
        def _(dve):
            nc.vector.memset(ones[:, :], 1.0).then_inc(filled, 1)
            nc.vector.memset(halves[:, :], 0.5).then_inc(filled, 1)
            nc.vector.memset(raw[:, :, :], 0.0).then_inc(filled, 1)
            dve.wait_ge(filled, 3)
            dve.wait_ge(turned, 1)
            for dx in range(3):
                for r in range(2):
                    for q in range(r, r + 3):
                        tap = (r + 2 - q) * 3 + dx
                        last = nc.vector.tensor_copy(raw[C * r:C * r + C, dx, C * q:C * q + C],
                                                     ps[C * r:C * r + C, tap // 8, (tap % 8) * C:(tap % 8 + 1) * C])
            last.then_inc(filled, 1)
            dve.wait_ge(filled, 4)
            flat = raw[:, :, :].rearrange("p a e -> p (a e)")
            nc.vector.scalar_tensor_tensor(w_junk[:, :], flat, 1.0, flat, ALU.mult, ALU.mult,
                                           accum_out=w_part[:, :]).then_inc(squared, 1)
            part = lambda i: taps[:, i, :, :].rearrange("p q o -> p (q o)")
            nc.vector.tensor_copy(part(0), raw[:, 0, :])
            nc.vector.tensor_copy(part(1), raw[:, 2, :]).then_inc(squared, 1)
            dve.wait_ge(squared, 2)
            nc.vector.tensor_tensor(raw[:, 0, :], raw[:, 0, :], raw[:, 2, :], ALU.add).then_inc(filled, 1)
            dve.wait_ge(filled, 5)
            nc.vector.tensor_scalar(raw[:, 0, :], raw[:, 0, :], 0.5, None, ALU.mult).then_inc(filled, 1)
            dve.wait_ge(filled, 6)
            nc.vector.scalar_tensor_tensor(part(2), raw[:, 1, :], 0.5, raw[:, 0, :], ALU.mult, ALU.add)
            nc.vector.scalar_tensor_tensor(part(3), raw[:, 1, :], 0.5, raw[:, 0, :], ALU.mult, ALU.subtract)
            dve.wait_ge(consts_in, 16)
            nc.vector.tensor_copy(fi_hi[:, :], con("fi")).then_inc(split, 1)
            dve.wait_ge(split, 1)
            nc.vector.tensor_tensor(fi_lo[:, :], con("fi"), fi_hi[:, :].bitcast(F32), ALU.subtract)
            dve.wait_ge(summed, 1)
            nc.vector.tensor_copy(w_sq[:, :], ps[:, 2, 0:1])


def weight_chunks(w_pair):
    return [w.rearrange("i o (m k) y -> m i o (k y)", k=KC) for w in w_pair]


def phase_a(nc, x, w_pos, modes_x, ps, con, con_in, ident, ones, mean0, dev0, room, w_first):
    NX = 8
    CB = 4
    CG = 16
    KB = 8
    NTR, NHG, NKB = C // CB, C // CG, NKY // KB
    FIRST = (0, 3)
    POOL_ADDS = (6, 9, 12, 15)
    DVE_ADDS = tuple(n for n in range(CPI) if n not in FIRST + POOL_ADDS)
    NDA, NPA = len(DVE_ADDS), len(POOL_ADDS)
    HDFT_AT = (1, 3, 6, 9)
    TURN_AT = (10, 11, 12, 13)
    SUMS_AT = 15
    RED_AT = 1
    x_v = x.rearrange("b (n r) (p j) c -> (b n) p r (j c)", r=RC, j=2)
    with ExitStack() as ctx:
        sb = lambda name, shape, dt=F32: ctx.enter_context(nc.sbuf_tensor(name, shape, dt))
        sem = lambda name: ctx.enter_context(nc.semaphore(name))
        xt = room[:, :].rearrange("p (u r e) -> p u r e", u=NX, r=RC)
        sq = sb("a_sq", [P, 3, RC * 2 * C])
        acc = sb("a_acc", [P, 2, RC * 2 * C])
        red = sb("a_red", [P, 2, C // GRP])
        red4 = sb("a_red4", [P, 2, C // GRP, GRP])
        gw = sb("a_gw", [P, C, P])
        gh = sb("a_gh", [P, C, P])
        xh = sb("a_xh", [P, NKY, C])
        xc = sb("a_xc", [P, NKX, NKY])
        tmp = sb("a_tmp", [P, 20])
        seed = sb("a_seed", [1, 8])
        x_in = [sem(f"x_in{u}") for u in range(NX)]
        dft_done, dft_evac = sem("dft_done"), sem("dft_evac")
        sq_done, sq_added, sq_pool_added = sem("sq_done"), sem("sq_added"), sem("sq_pool_added")
        acc_summed = [sem(f"acc_summed{i}") for i in range(2)]
        turned, gh_even, gh_odd = sem("gw_turned"), sem("gh_even"), sem("gh_odd")
        hdft_done, xh_evac = sem("hdft_done"), sem("xh_evac")
        mode_turned, xc_evac = sem("mode_turned"), sem("xc_evac")
        red_ready, sums_done, stats_step = sem("red_ready"), sem("sums_done"), sem("stats_step")
        xc_ready, xc_stored = sem("xc_ready"), sem("xc_stored")
        block = ctx.enter_context(nc.Block())
        STATS = 6
        fw = con("fw").rearrange("p (j k) -> p j k", j=2)
        fh = con("fh").rearrange("p (g f k) -> p g f k", g=2, f=2)

        @block.sync
        def _(sync):
            def load(n, u):
                for half in (slice(0, RC // 2), slice(RC // 2, RC)):
                    sync.dma_start(xt[:, u, half, :], x_v[n][:, half]).then_inc(x_in[u], 16)

            for u in range(NX):
                load(u, u)
            with sync.Fori(0, NCH // NX - 1) as t:
                for u in range(NX):
                    sync.wait_ge(dft_done, t * NX + (u + 1))
                    sync.wait_ge(sq_done, t * NX + (u + 1))
                    load(t * NX + (u + NX), u)
            sync.wait_ge(dft_done, NCH)
            sync.wait_ge(sq_done, NCH)
            first = room[:, :].rearrange("p (u o m) -> p u o m", u=2, o=C)
            w_v = weight_chunks(w_pos)
            for u in range(2):
                for ri in range(2):
                    sync.dma_start(first[C * ri:C * ri + C, u, :, :], w_v[ri][u]).then_inc(w_first[u], 16)

        @block.tensor
        def _(pe):
            def over_h(b, q):
                pe.wait_ge(gh_even, b * (NTR // 2) + NTR // 2)
                pe.wait_ge(gh_odd, b * (NTR // 2) + NTR // 2)
                pe.wait_ge(xh_evac, b * NHG + (q + 1))
                pe.wait_ge(xc_ready, b + GIVEN)
                for n, (g, f) in enumerate(((0, 0), (0, 1), (1, 0), (1, 1))):
                    lo = 64 * g + 32 * f
                    last = nc.tensor.matmul(ps[:, 6 + q % 2, :], fh[:, g, f, :],
                                            gh[:, CG * q:CG * (q + 1), lo:lo + NKY], start=(n == 0), stop=(n == 3))
                last.then_inc(hdft_done, 1)

            def turn_modes(b, q):
                pe.wait_ge(xh_evac, b * NHG + (NHG + 2))
                pe.wait_ge(xc_evac, b * NKB + (q + 1))
                for i in range(KB // 2):
                    ky = KB * q + 2 * i
                    last = nc.tensor.transpose(ps[:, 2 + q % 2, i * P:(i + 1) * P],
                                               xh[:, ky:ky + 2, :].rearrange("p y c -> p (y c)"), ident)
                last.then_inc(mode_turned, 1)

            def sums(b):
                pe.wait_ge(xc_evac, b * NKB + (NKB + 2))
                pe.wait_ge(red_ready, b + 1 + GIVEN)
                nc.tensor.matmul(ps[:, 6, 0:1], red4[:, :, :, :].rearrange("p a g e -> p (a g e)"),
                                 ones[:, 0:1], start=True, stop=True)
                nc.tensor.matmul(ps[:, 6, 1:2], con("pair_re"), xc[:, 0, 0:1],
                                 start=True, stop=True).then_inc(sums_done, 1)

            def rest(b, n):
                if n in HDFT_AT:
                    over_h(b, HDFT_AT.index(n))
                if n in TURN_AT:
                    turn_modes(b, TURN_AT.index(n))
                if n == SUMS_AT:
                    sums(b)

            def image(b, first=False):
                for n in range(CPI):
                    pe.wait_ge(x_in[n % NX], (b * (CPI // NX) + n // NX) * 32 + 32)
                    pe.wait_ge(dft_evac, b * CPI + (n + 1))
                    for j in range(2):
                        for g in range(2):
                            last = nc.tensor.matmul(ps[64 * g:64 * g + 64, n % 2, :], fw[:, j, :],
                                                    xt[:, n % NX, 8 * g:8 * g + 8, C * j:C * j + C],
                                                    start=(j == 0), stop=(j == 1))
                    last.then_inc(dft_done, 1)
                    if not first:
                        rest(b - 1, n)
                pe.wait_ge(dft_evac, b * CPI + (CPI + 2))
                for q in range(NTR):
                    if q >= 4:
                        pe.wait_ge((gh_even, gh_odd)[q % 2], b * (NTR // 2) + ((q - 4) // 2 + 1))
                    for i in range(CB):
                        last = nc.tensor.transpose(ps[:, 2 + q % 4, i * P:(i + 1) * P], gw[:, CB * q + i, :], ident)
                    last.then_inc(turned, 1)

            image(0, first=True)
            with pe.Fori(1, B) as b:
                image(b)
            for n in range(CPI):
                rest(B - 1, n)

        @block.scalar
        def _(act):
            def take_modes(b, q):
                if q == 0:
                    act.wait_ge(xc_stored, b * 16 + 16)
                act.wait_ge(mode_turned, b * NKB + (q + 1) + GIVEN)
                bank = ps[:, 2 + q % 2, :].rearrange("p (y f k) -> p f k y", y=KB // 2, f=2)
                for f in range(2):
                    for e in range(2):
                        last = nc.scalar.activation(xc[C * f:C * f + C, :, KB * q + e:KB * (q + 1):2],
                                                    bank[C * e:C * e + C, f, :, :], ACT.Copy)
                last.then_inc(xc_evac, 1)

            def image(b, first=False):
                for n in range(CPI):
                    act.wait_ge(x_in[n % NX], (b * (CPI // NX) + n // NX) * 32 + 32)
                    if n in FIRST:
                        act.wait_ge(acc_summed[FIRST.index(n)], b + GIVEN)
                        to = acc[:, FIRST.index(n), :]
                    elif n in POOL_ADDS:
                        act.wait_ge(sq_pool_added, b * NPA + POOL_ADDS.index(n) + GIVEN)
                        to = sq[:, 2, :]
                    else:
                        k = DVE_ADDS.index(n)
                        act.wait_ge(sq_added, b * NDA + max(k - 1, 0) + GIVEN)
                        to = sq[:, k % 2, :]
                    nc.scalar.activation(to, xt[:, n % NX, :, :].rearrange("p r e -> p (r e)"),
                                         ACT.Square).then_inc(sq_done, 1)
                    if not first and n - 1 in TURN_AT:
                        take_modes(b - 1, TURN_AT.index(n - 1))
                act.wait_ge(hdft_done, b * NHG + GIVEN)
                for q in range(0, NTR, 2):
                    act.wait_ge(turned, b * NTR + (q + 1) + GIVEN)
                    nc.scalar.activation(gh[:, CB * q:CB * (q + 1), :].rearrange("p c k -> p (c k)"),
                                         ps[:, 2 + q % 4, :], ACT.Copy).then_inc(gh_even, 1)

            image(0, first=True)
            with act.Fori(1, B) as b:
                image(b)
            for q in range(NKB):
                take_modes(B - 1, q)

        @block.vector
        def _(dve):
            def add(b, n):
                if n in DVE_ADDS:
                    k = DVE_ADDS.index(n)
                    dve.wait_ge(sq_done, b * CPI + (n + 1))
                    dve.wait_ge(sq_added, b * NDA + k + GIVEN)
                    nc.vector.tensor_tensor(acc[:, 0, :], acc[:, 0, :], sq[:, k % 2, :], ALU.add).then_inc(sq_added, 1)

            def reduce(b, i):
                if i == 0:
                    dve.wait_ge(sq_added, b * NDA + NDA + GIVEN)
                    dve.wait_ge(red_ready, b + GIVEN)
                else:
                    dve.wait_ge(sq_pool_added, b * NPA + NPA + GIVEN)
                nc.vector.tensor_reduce(red[:, i, :], acc[:, i, :].rearrange("p (m g e) -> p g m e", g=C // GRP, e=GRP),
                                        AX.XY, ALU.add).then_inc(acc_summed[i], 1)

            def group(b):
                for i in range(2):
                    dve.wait_ge(acc_summed[i], b + 1 + GIVEN)
                dve.wait_ge(sums_done, b + GIVEN)
                for a in range(2):
                    part = lambda i: red[:, i, :].unsqueeze(2).broadcast_to([P, C // GRP, GRP])
                    last = nc.vector.tensor_tensor(red4[:, a, :, :], part(0), part(1), ALU.add)
                last.then_inc(red_ready, 1)

            def take_h(b, q):
                if q == 0:
                    dve.wait_ge(mode_turned, b * NKB + GIVEN)
                dve.wait_ge(hdft_done, b * NHG + (q + 1) + GIVEN)
                nc.vector.tensor_copy(xh[:, :, CG * q:CG * (q + 1)],
                                      ps[:, 6 + q % 2, :].rearrange("p (c y) -> p y c", c=CG)).then_inc(xh_evac, 1)

            def stats(b):
                dve.wait_ge(sums_done, b + 1 + GIVEN)
                step = Chain(dve, stats_step, b * STATS, STATS)
                step(nc.vector.tensor_copy(tmp[:, 0:2], ps[:, 6, 0:2]))
                step(nc.vector.tensor_scalar(mean0[:, bass.ds(b, 1)], tmp[:, 1:2], 1.0 / NORM, None, ALU.mult))
                step(nc.vector.tensor_tensor(tmp[:, 2:3], tmp[:, 1:2], mean0[:, bass.ds(b, 1)], ALU.mult))
                step(nc.vector.tensor_tensor(dev0[:, bass.ds(b, 1)], tmp[:, 0:1], tmp[:, 2:3], ALU.subtract))
                step(nc.vector.tensor_scalar(tmp[:, 3:4], mean0[:, bass.ds(b, 1)], float(-NPIX), None, ALU.mult))
                step(nc.vector.tensor_tensor(xc[0:C, 0, 0:1], xc[0:C, 0, 0:1], tmp[0:C, 3:4], ALU.add))
                step.end()
                nc.vector.memset(tmp[:, 2:3], 0.0).then_inc(xc_ready, 1)

            def rest(b, n):
                if n == RED_AT:
                    reduce(b, 1)
                    group(b)
                if n - 1 in HDFT_AT:
                    take_h(b, HDFT_AT.index(n - 1))
            def image(b, first=False):
                dve.wait_ge(turned, b * NTR + GIVEN)
                for n in range(CPI):
                    dve.wait_ge(dft_done, b * CPI + (n + 1))
                    nc.vector.tensor_copy(gw[:, :, 8 * n:8 * n + 8],
                                          ps[:, n % 2, :].rearrange("p (r c) -> p c r", c=C)).then_inc(dft_evac, 1)
                    if 1 <= n < CPI - 1:
                        add(b, n - 1)
                    if not first:
                        rest(b - 1, n)
                dve.wait_ge(hdft_done, b * NHG + GIVEN)
                for q in range(1, NTR, 2):
                    dve.wait_ge(turned, b * NTR + (q + 1) + GIVEN)
                    nc.vector.tensor_copy(gh[:, CB * q:CB * (q + 1), :].rearrange("p c k -> p (c k)"),
                                          ps[:, 2 + q % 4, :]).then_inc(gh_odd, 1)
                add(b, CPI - 2)
                if not first:
                    stats(b - 1)
                reduce(b, 0)

            for i, (s, given) in enumerate(((dft_evac, 2), (xh_evac, 2), (xc_evac, 2), (sq_added, GIVEN),
                                            (sq_pool_added, GIVEN), (acc_summed[0], GIVEN), (acc_summed[1], GIVEN),
                                            (hdft_done, GIVEN), (turned, GIVEN), (sums_done, GIVEN), (mode_turned, GIVEN),
                                            (red_ready, GIVEN), (xc_ready, GIVEN))):
                nc.vector.memset(tmp[:, 4 + i:5 + i], 0.0).then_inc(s, given)
            image(0, first=True)
            with dve.Fori(1, B) as b:
                image(b)
            for n in range(CPI):
                rest(B - 1, n)
            stats(B - 1)

        @block.gpsimd
        def _(pool):
            def adds(b):
                for k, n in enumerate(POOL_ADDS):
                    pool.wait_ge(sq_done, b * CPI + (n + 1))
                    pool.wait_ge(sq_pool_added, b * NPA + k + GIVEN)
                    nc.gpsimd.tensor_tensor(acc[:, 1, :], acc[:, 1, :], sq[:, 2, :], ALU.add).then_inc(sq_pool_added, 1)

            def store(b):
                pool.wait_ge(xc_ready, b + 1 + GIVEN)
                pool.dma_start(modes_x[b], xc[:, :, :].rearrange("p k y -> p (k y)")).then_inc(xc_stored, 16)

            pool.dma_start(seed[:, :], con_in).then_inc(xc_stored, 16)
            adds(0)
            with pool.Fori(1, B) as b:
                adds(b)
                store(b - 1)
            store(B - 1)
            pool.wait_ge(xc_stored, B * 16 + 16)


def phase_m(nc, w_pos, w_neg, modes_x, modes_o, ps, con, con_in, dev0, room, w_first):
    NM = NKX // KC
    NW = 4
    TQ = 4
    KT = NKY // TQ
    with ExitStack() as ctx:
        sb = lambda name, shape, dt=F32: ctx.enter_context(nc.sbuf_tensor(name, shape, dt))
        sem = lambda name: ctx.enter_context(nc.semaphore(name))
        wt_first = room[:, :].rearrange("p (u o m) -> p u o m", u=2, o=C)
        wt_rest = sb("m_w", [P, NW - 2, C, MC])
        wt = lambda u: wt_first[:, u] if u < 2 else wt_rest[:, u - 2]
        xs = sb("m_x", [P, 2, B, MC])
        st = sb("m_s", [P, 2, MC, 4 * B])
        ot = sb("m_o", [P, 2, KC, KT * C])
        seed = sb("m_seed", [1, 2, 8])
        rstd = sb("m_rstd", [P, 6, B])
        w_in = w_first + [sem(f"w_in{u}") for u in range(2, NW)]
        xs_in = [sem(f"xs_in{u}") for u in range(2)]
        s_ready, o_done, o_evac, norm_step = sem("s_ready"), sem("o_done"), sem("o_evac"), sem("norm_step")
        var_ready, sqrt_done = sem("m_var_ready"), sem("m_sqrt_done")
        o_stored = [sem(f"o_stored{u}") for u in range(2)]
        block = ctx.enter_context(nc.Block())
        xs_v = modes_x.rearrange("b p (m e) -> m p b e", e=MC)
        w_v = [weight_chunks(pair) for pair in (w_pos, w_neg)]
        o_v = modes_o.rearrange("q b (m k) (t e) -> m t (q b) k e", k=KC, t=TQ)
        HALF = NM // 2

        @block.sync
        def _(sync):
            def load_w(sign, m_half, u):
                for ri in range(2):
                    sync.dma_start(wt(u)[C * ri:C * ri + C, :, :], w_v[sign][ri][m_half]).then_inc(w_in[u], 16)

            def load_x(m, u):
                sync.dma_start(xs[:, u, :, :], xs_v[m]).then_inc(xs_in[u], 16)

            def multiplied(n):
                sync.wait_ge(o_done, n * KC + (KC + GIVEN))

            for u in range(NW):
                if u < 2:
                    load_x(u, u)
                else:
                    load_w(0, u, u)
            for u in range(NW):
                multiplied(u + 1)
                load_x(u + 2, u % 2)
                load_w(0, u + NW, u)
            with sync.Fori(1, HALF // NW + 1) as t:
                for u in range(NW):
                    multiplied(t * NW + (u + 1))
                    load_x(t * NW + (u + 2), u % 2)
                    load_w(1, (t - 1) * NW + u, u)
            for u in range(2):
                multiplied(NM - NW + u + 1)
                load_x(NM - NW + u + 2, u % 2)

        @block.tensor
        def _(pe):
            with pe.Fori(0, NM // NW) as t:
                for w in range(NW):
                    u = w % 2
                    pe.wait_ge(w_in[w], t * 32 + 32)
                    pe.wait_ge(s_ready, t * NW + (w + 1))
                    for k in range(KC):
                        pe.wait_ge(o_evac, t * (NW * KC) + (KC * w + k + 1))
                        for i in range(KT):
                            for tq in range(TQ):
                                mode = k * NKY + tq * KT + i
                                last = nc.tensor.matmul(ps[32 * tq:32 * tq + 32, KC * u + k, C * i:C * i + C],
                                                        st[:, u, mode, :], wt(w)[:, :, mode], start=True, stop=True)
                        last.then_inc(o_done, 1)

        @block.vector
        def _(dve):
            nc.vector.memset(rstd[:, 5, 0:1], 0.0).then_inc(o_done, KC + GIVEN)
            nc.vector.memset(rstd[:, 5, 1:2], 0.0).then_inc(o_evac, 8)
            step = Chain(dve, norm_step, 0, 10)
            step(nc.vector.memset(st[:, :, :, 3 * B:], 0.0))
            step(nc.vector.tensor_scalar(rstd[:, 3, :], dev0[:, :], 1.0 / NORM, 0.0, ALU.mult, ALU.max))
            step(nc.vector.tensor_scalar(rstd[:, 3, :], rstd[:, 3, :], EPS, None, ALU.add))
            nc.vector.memset(rstd[:, 5, 0:1], 0.0).then_inc(var_ready, 1)
            dve.wait_ge(sqrt_done, 1)
            step(nc.vector.reciprocal(rstd[:, 0, :], rstd[:, 4, :]))
            step(nc.vector.tensor_tensor(rstd[:, 0, :], rstd[:, 0, :], rstd[:, 3, :], ALU.mult))
            step(nc.vector.tensor_tensor(rstd[:, 0, :], rstd[:, 0, :], rstd[:, 4, :], ALU.add))
            step(nc.vector.tensor_scalar(rstd[:, 5, :], rstd[:, 0, :], 0.5, None, ALU.mult))
            step(nc.vector.reciprocal(rstd[:, 0, :], rstd[:, 5, :]))
            step(nc.vector.tensor_scalar(rstd[:, 1, :], rstd[:, 0, :], con("sgn"), None, ALU.mult))
            step(nc.vector.tensor_scalar(rstd[:, 2, :], rstd[:, 1, :], -1.0, None, ALU.mult))
            step.end()
            with dve.Fori(0, NM // 2) as t:
                for u in range(2):
                    dve.wait_ge(xs_in[u], t * 16 + 16)
                    dve.wait_ge(o_done, t * (2 * KC) + KC * u + GIVEN)
                    cols = lambda q: st[:, u, :, q * B:(q + 1) * B].rearrange("p m b -> p b m")
                    scale = lambda row: rstd[:, row, :].unsqueeze(2).broadcast_to([P, B, MC])
                    nc.vector.tensor_tensor(cols(0), xs[:, u, :, :], scale(1), ALU.mult)
                    nc.vector.tensor_tensor(cols(2), xs[:, u, :, :], scale(2), ALU.mult)
                    nc.vector.tensor_tensor(cols(1)[C:P], xs[0:C, u, :, :], scale(0)[0:C], ALU.mult)
                    nc.vector.tensor_tensor(cols(1)[0:C], xs[C:P, u, :, :], scale(0)[C:P], ALU.mult).then_inc(s_ready, 1)

        @block.scalar
        def _(act):
            for u in range(2):
                act.dma_start(seed[:, u, :], con_in).then_inc(o_stored[u], 16)
            act.wait_ge(var_ready, 1)
            nc.scalar.activation(rstd[:, 4, :], rstd[:, 3, :], ACT.Sqrt).then_inc(sqrt_done, 1)
            with act.Fori(0, NM // 2) as t:
                for u in range(2):
                    act.wait_ge(o_stored[u], t * 64 + 16)
                    for k in range(KC):
                        act.wait_ge(o_done, t * (2 * KC) + (KC * u + k + 1 + KC) + GIVEN)
                        nc.scalar.activation(ot[:, u, k, :], ps[:, KC * u + k, :], ACT.Copy).then_inc(o_evac, 1)
                    act.wait_ge(o_evac, t * (2 * KC) + (KC * u + KC + 8))
                    for tq in range(TQ):
                        act.dma_start(o_v[t * 2 + u, tq], ot[32 * tq:32 * tq + 3 * B, u, :, :]).then_inc(o_stored[u], 16)
            for u in range(2):
                act.wait_ge(o_stored[u], NM // 2 * 64 + 16)


def phase_b(nc, x, out, modes_x, modes_o, ps, con, con_in, ident, ones, halves, taps, w_sq, mean0, dev0, fi_hi, fi_lo):
    RB = 8
    NB = H // RB
    BB = 4
    NIT = NB // BB
    OB = 2
    NY = H // 4
    RING = 16
    ZW = W + 2
    PH = P
    PARTS = (2, 3, 0, 1)
    NP = len(PARTS)
    NV = NP - 1
    NOT = NKY // 8
    NTB = C // 4
    NF = 3
    Y0, S0, CV = 0, 2, 4
    x_v = x.rearrange("b (n r) (p j) c -> b n p j r c", r=RC, j=2)
    out_v = out.rearrange("b (n r) (p j) c -> b n p r (j c)", r=RB, j=2)
    with ExitStack() as ctx:
        sb = lambda name, shape, dt=F32: ctx.enter_context(nc.sbuf_tensor(name, shape, dt))
        sem = lambda name: ctx.enter_context(nc.semaphore(name))
        om = sb("b_om", [P, 2, NKY, C])
        xm = sb("b_xm", [P, NKX, NKY])
        oc = sb("b_oc", [P, NKX, NKY])
        sc = sb("b_sc", [P, 48])
        th = sb("b_th", [P, H, C], F32R)
        ts = sb("b_ts", [P, 4, RB, C], F32R)
        yb = sb("b_yb", [P, 2, 2, ZW])
        vb = sb("b_vb", [P, 4, 2, NP, PH])
        xt = sb("b_xt", [P, 2, 2, RC, C])
        zh = sb("b_zh", [P, RING, NP, PH], F16)
        zl = sb("b_zl", [P, RING, NP, PH], F16)
        wh = sb("b_wh", [P, NP, 4, C], F16)
        wl = sb("b_wl", [P, NP, 4, C], F16)
        next_wh = sb("b_next_wh", [P, NP, 4, C], F16)
        next_wl = sb("b_next_wl", [P, NP, 4, C], F16)
        wc = sb("b_wc", [P, 2, C])
        m1 = sb("b_m1", [P, RB * C])
        diag = sb("b_diag", [P, C])
        seed = sb("b_seed", [1, OB, 8])
        mrow = sb("b_mrow", [P, C])
        next_mrow = sb("b_next_mrow", [P, C])
        ob = sb("b_ob", [P, OB, RB, 2 * C])
        col = {n: sc[:, i:i + 1] for i, n in enumerate(
            ("a_rest", "a_ky0", "a_mirror", "a_dc", "part", "dc", "mean", "mean_d", "var", "sd", "sigma", "rstd",
             "w1", "w2", "fro", "froot", "f", "inv_f", "sigma_f", "neg_inv_f", "next_rstd", "next_inv_f", "next_neg_inv_f"))}
        om_in, xm_in = sem("om_in"), sem("xm_in")
        x_in = [sem(f"bx_in{u}") for u in range(2)]
        oc_turned, oc_evac = sem("oc_turned"), sem("oc_evac")
        part_ready, group_done, var_ready, sd_ready = map(sem, ("part_ready", "group_done", "b_var_ready", "sd_ready"))
        sig_done, fro_ready, froot_ready = map(sem, ("sig_done", "fro_ready", "froot_ready"))
        mean_ready, mrow_done, om_fixed, next_ready = map(sem, ("mean_ready", "mrow_done", "om_fixed", "next_ready"))
        f_ready, next_wh_ready = sem("f_ready"), sem("next_wh_ready")
        rstd_ready, scale_ready, wh_ready, wl_ready = map(sem, ("rstd_ready", "scale_ready", "wh_ready", "wl_ready"))
        t_done, t_hi, t_lo, ts_ready = map(sem, ("t_done", "t_hi", "t_lo", "ts_ready"))
        y_done, y_evac, v_sum, v_diff = map(sem, ("y_done", "y_evac", "v_sum", "v_diff"))
        m1_evac, m1_ready = sem("m1_evac"), sem("m1_ready")
        z_hi, z_lo, conv_done, out_evac = map(sem, ("z_hi", "z_lo", "conv_done", "out_evac"))
        out_stored = [sem(f"out_stored{u}") for u in range(OB)]
        bstep, cleared = sem("bstep"), sem("cleared")
        block = ctx.enter_context(nc.Block())
        YG = 8
        YE = 2
        SLOT = 4
        CG = NP + 1
        STEPS = 36
        y_order = lambda last: [[n for n in (2 * kk + 3, 2 * kk + 4) if not (last and n >= 2 * BB)] for kk in range(BB)]
        t_banks_of = lambda bn: 6 if isinstance(bn, int) and bn == 0 else 2
        T_AT = {(kk, i): [5 * kk + i + 1] for kk in range(BB - 1) for i in range(-1, NP)}
        T_AT[BB - 2, NP - 1].append(NTB - 1)

        @block.sync
        def _(sync):
            def load_x(b, n, u):
                for j in range(2):
                    sync.dma_start(xt[:, u, j, :, :], x_v[b, n][:, j]).then_inc(x_in[u], 16)

            def body(b, it, last=False, more=True):
                for kk in range(BB):
                    if kk % 2 == 0 and not (last and not more):
                        sync.wait_ge(y_done, b * NY + it * (2 * BB) + (2 * kk + 4 + YG))
                        if last:
                            load_x(b + 1, kk // 2, kk // 2)
                        else:
                            load_x(b, it * 2 + (kk // 2 + 2), kk // 2)
                    sync.wait_ge(out_evac, b * (NV * NB) + it * (NV * BB) + NV * (kk + 1) + NV)
                    sync.dma_start(out_v[b, it * BB + kk], ob[:, kk % OB, :, :]).then_inc(out_stored[kk % OB], 16)

            def image(b, more=True):
                with sync.Fori(0, NIT - 1) as it:
                    body(b, it)
                body(b, NIT - 1, last=True, more=more)

            for u in range(OB):
                sync.dma_start(seed[:, u, :], con_in).then_inc(out_stored[u], 16)
            sync.wait_ge(om_in, 64)
            for u in range(2):
                load_x(0, u, u)
            with sync.Fori(0, B - 1) as b:
                image(b)
            image(B - 1, more=False)
            for u in range(OB):
                sync.wait_ge(out_stored[u], B * (NB // OB) * 16 + 16)

        @block.tensor
        def _(pe):
            def turn_modes(bn, q):
                if q == 0:
                    pe.wait_ge(om_in, bn * 64 + 64)
                    pe.wait_ge(t_lo, bn * NTB + GIVEN)
                if q >= 2:
                    pe.wait_ge(oc_evac, bn * NOT + (q - 1))
                for i in range(4):
                    ky = 8 * q + 2 * i
                    last = nc.tensor.transpose(ps[:, S0 + q % 2, i * P:(i + 1) * P],
                                               om[:, 0, ky:ky + 2, :].rearrange("p y c -> p (y c)"), ident)
                last.then_inc(oc_turned, 1)

            def group_sums(bn):
                pe.wait_ge(part_ready, bn + 1 + GIVEN)
                nc.tensor.matmul(ps[:, S0, 0:1], con("pair_all"), col["part"], start=True, stop=True)
                nc.tensor.matmul(ps[:, S0, 1:2], con("pair_re"), col["dc"], start=True, stop=True).then_inc(group_done, 1)

            def norm_sums(bn):
                pe.wait_ge(var_ready, bn + 1)
                nc.tensor.matmul(ps[:, S0, 2:3], halves[:, :], col["var"], start=True, stop=True).then_inc(sig_done, 1)
                pe.wait_ge(mean_ready, bn + 1)
                nc.tensor.matmul(ps[:, S0 + 1, 0:C], ones[:, :], diag[:, :], start=True, stop=True).then_inc(mrow_done, 1)

            def t_bank(bn, q):
                if q == 0:
                    pe.wait_ge(om_fixed, bn + 1)
                    pe.wait_ge(fro_ready, bn + 1)
                if q >= t_banks_of(bn):
                    pe.wait_ge(t_lo, bn * NTB + (q - t_banks_of(bn) + 1) + GIVEN)
                for i in range(2):
                    for half in range(2):
                        c = 2 * q + i + half * (C // 2)
                        last = nc.tensor.matmul(ps[64 * half:64 * half + 64, S0 + q % t_banks_of(bn), i * H:(i + 1) * H],
                                                om[:, :, :, c].rearrange("p f y -> p (f y)"), con("eh"),
                                                start=True, stop=True)
                last.then_inc(t_done, 1)

            def y_bank(b, it, n):
                u = (n // 4) % 2
                if n % 4 == 0:
                    pe.wait_ge(x_in[u], b * (CPI // 2 * 32) + it * 32 + (n // 8 * 32 + 32))
                pe.wait_ge(ts_ready, b * NB + it * BB + (n // 2 + 1) + GIVEN)
                pe.wait_ge(y_evac, b * NY + it * (2 * BB) + (n + 1))
                bank = Y0 + n % 2
                for k in range(2):
                    r = (n % 4) * 4 + 2 * k
                    for jj in range(2):
                        j = 1 - jj
                        nc.tensor.matmul(ps[:, bank, k * W + jj * P:k * W + (jj + 1) * P],
                                         xt[:, u, j, r:r + 2, :].rearrange("p r c -> p (r c)"), ident, is_transpose=True,
                                         start=(k == 0 and jj == 0), stop=False, skip_group_check=True)
                for k in range(2):
                    r = (n % 2) * 4 + 2 * k
                    for f in (fi_hi, fi_lo):
                        last = nc.tensor.matmul(ps[:, bank, k * W:(k + 1) * W],
                                                ts[:, (n // 2) % 4, r:r + 2, :].rearrange("p r c -> p (r c)"), f[:, :],
                                                start=False, stop=(f is fi_lo and k == 1), skip_group_check=True)
                last.then_inc(y_done, 1)

            def product(b, it, kk, i, first_block, last_block):
                blocks = b * NB + it * BB + kk
                if i == 0:
                    pe.wait_ge(z_lo, b * NY + it * (2 * BB) + (2 * kk + (2 if last_block else 3)) + SLOT)
                    if first_block:
                        pe.wait_ge(wh_ready, b + 1)
                        pe.wait_ge(wl_ready, b + 1)
                    pe.wait_ge(m1_evac, blocks + GIVEN)
                else:
                    pe.wait_ge(out_evac, blocks * NV + i)
                pairs = range(4 * kk - (0 if first_block else 1), 4 * kk + (4 if last_block else 5))
                pairs = sorted(pairs, key=lambda q: not 4 * kk <= q < 4 * kk + 4)
                part = PARTS[i]
                n, total = 0, 3 * len(pairs)
                for z, w in ((zh, wh), (zl, wh), (zh, wl)):
                    for pair in pairs:
                        row = 2 * pair - 1 - RB * kk
                        q0, q1 = max(0, -row), min(4, RB - row)
                        last = nc.tensor.matmul(
                            ps[:, CV + i, (row + q0) * C:(row + q1) * C],
                            z[:, pair % RING, part, :],
                            w[:, part, q0:q1, :].rearrange("p q o -> p (q o)"),
                            start=(n == 0), stop=(n == total - 1), skip_group_check=True)
                        n += 1
                last.then_inc(conv_done, 1)

            def body(b, it, number=None, more=True):
                last = number == NIT - 1
                for kk, banks in enumerate(y_order(last)):
                    for n in banks:
                        y_bank(b, it, n)
                    at = (number, kk) if more else None
                    for i in range(-1, NP):
                        if i >= 0:
                            product(b, it, kk, i, number == 0 and kk == 0, last and kk == BB - 1)
                        if i == 1:
                            if at in ((0, 2), (0, 3)):
                                turn_modes(b + 1, 2 * kk - 4)
                                turn_modes(b + 1, 2 * kk - 3)
                            if at == (2, 0):
                                group_sums(b + 1)
                            if at == (2, 1):
                                norm_sums(b + 1)
                        if last and more:
                            for q in T_AT.get((kk, i), ()):
                                t_bank(b + 1, q)
                            if kk == BB - 1:
                                for n in {1: (0, 1), 2: (2,)}.get(i, ()):
                                    y_bank(b + 1, 0, n)

            def image(b, more=True):
                body(b, 0, 0, more)
                body(b, 1, 1, more)
                body(b, 2, 2, more)
                with pe.Fori(3, NIT - 1) as it:
                    body(b, it)
                body(b, NIT - 1, NIT - 1, more)

            for q in range(NOT):
                turn_modes(0, q)
            group_sums(0)
            norm_sums(0)
            for q in range(NTB):
                t_bank(0, q)
            for n in range(NF):
                y_bank(0, 0, n)
            with pe.Fori(0, B - 1) as b:
                image(b)
            image(B - 1, more=False)

        def z_slot(t, n):
            return t[:, (2 * n) % RING:(2 * n) % RING + 2, :, :].rearrange("p k v e -> p (k v e)")

        def v_slot(n):
            return vb[:, n % 4, :, :, :].rearrange("p k v e -> p (k v e)")

        @block.scalar
        def _(act):
            def load_om(bn):
                act.wait_ge(t_done, bn * NTB + GIVEN)
                for form in range(2):
                    for ri in range(2):
                        act.dma_start(om[NKX * ri:NKX * ri + NKX, form, :, :].rearrange("p y o -> p (y o)"),
                                      modes_o[form + ri, bn]).then_inc(om_in, 16)

            def load_xm(bn):
                act.wait_ge(part_ready, bn + GIVEN)
                act.dma_start(xm[:, :, :].rearrange("p k y -> p (k y)"), modes_x[bn]).then_inc(xm_in, 16)

            def take_modes(bn, q):
                if q == 0:
                    act.wait_ge(part_ready, bn + GIVEN)
                act.wait_ge(oc_turned, bn * NOT + (q + 1))
                bank = ps[:, S0 + q % 2, :].rearrange("p (y f k) -> p f k y", y=4, f=2)
                for f in range(2):
                    last = nc.scalar.activation(oc[C * f:C * f + C, :, 8 * q:8 * q + 8:2], bank[0:C, f, :, :], ACT.Copy)
                for f in range(2):
                    last = nc.scalar.activation(oc[C * f:C * f + C, :, 8 * q + 1:8 * q + 8:2], bank[C:P, f, :, :], ACT.Copy)
                last.then_inc(oc_evac, 1)

            def roots(bn):
                act.wait_ge(var_ready, bn + 1)
                nc.scalar.activation(col["sd"], col["var"], ACT.Sqrt).then_inc(sd_ready, 1)
                act.wait_ge(fro_ready, bn + 1)
                nc.scalar.activation(col["froot"], col["fro"], ACT.Sqrt).then_inc(froot_ready, 1)

            def high_weights(bn):
                act.wait_ge(f_ready, bn + 1)
                if not isinstance(bn, int):
                    act.wait_ge(wh_ready, bn)
                nc.scalar.activation(next_wh[:, :, :, :], taps[:, :, :, :], ACT.Copy, scale=col["f"]).then_inc(next_wh_ready, 1)

            def t_high(bn, q):
                if q == 0:
                    act.wait_ge(ts_ready, bn * NB + GIVEN)
                act.wait_ge(t_done, bn * NTB + (q + 1) + GIVEN)
                for half in range(2):
                    c = 2 * q + half * (C // 2)
                    last = nc.scalar.activation(
                        th[64 * half:64 * half + 64, :, c:c + 2],
                        ps[64 * half:64 * half + 64, S0 + q % t_banks_of(bn), :].rearrange("p (c h) -> p h c", c=2),
                        ACT.Copy)
                last.then_inc(t_hi, 1)

            def rows(b, it, m):
                act.wait_ge(y_done, b * NY + it * (2 * BB) + (2 * m + 2))
                nc.scalar.activation(ts[:, m % 4, :, :], th[:, bass.ds(it * (BB * RB) + m * RB, RB), :].bitcast(F32), ACT.Copy)\
                    .then_inc(ts_ready, 1)

            def first_rows(bn, m):
                if m == 0:
                    act.wait_ge(t_lo, bn * NTB + NTB + GIVEN)
                rows(bn, 0, m)

            def take_y(b, it, n):
                act.wait_ge(y_done, b * NY + it * (2 * BB) + (n + 1 + YG))
                for s in (v_sum, v_diff):
                    act.wait_ge(s, b * NY + it * (2 * BB) + (n - 1 + SLOT))
                nc.scalar.activation(yb[:, n % 2, :, 1:1 + W], ps[:, Y0 + n % 2, :].rearrange("p (k w) -> p k w", k=2),
                                     ACT.Copy, scale=col["rstd"]).then_inc(y_evac, 1)

            def high(b, it, n, blocks):
                for s in (v_sum, v_diff):
                    act.wait_ge(s, b * NY + it * (2 * BB) + (n + 1 + SLOT))
                act.wait_ge(conv_done, blocks * NP + CG)
                nc.scalar.activation(z_slot(zh, n), v_slot(n), ACT.Copy).then_inc(z_hi, 1)

            def take_m1(b, it, kk):
                act.wait_ge(conv_done, b * (NP * NB) + it * (NP * BB) + (NP * kk + 1) + CG)
                act.wait_ge(out_evac, b * (NV * NB) + it * (NV * BB) + NV * kk + 1)
                nc.scalar.activation(m1[:, :], ps[:, CV, :], ACT.Copy, scale=col["inv_f"]).then_inc(m1_evac, 1)

            def low_weights(b):
                act.wait_ge(next_ready, b + 1)
                act.wait_ge(conv_done, b * (NP * NB) + CG)
                nc.scalar.activation(wl[:, :, :, :], next_wl[:, :, :, :], ACT.Copy).then_inc(wl_ready, 1)

            def body(b, it, number=None, more=True):
                last = number == NIT - 1
                for kk, banks in enumerate(y_order(last)):
                    t_banks = lambda i: T_AT.get((kk, i), ()) if last and more else ()
                    blocks = b * NB + it * BB + (kk - 1)
                    if number == 0 and kk == 0:
                        low_weights(b)
                    if not (last and kk + 3 >= BB):
                        rows(b, it, kk + 3)
                    for n in banks:
                        take_y(b, it, n)
                    for q in t_banks(-1):
                        t_high(b + 1, q)
                    if number == 0 and kk == 0:
                        act.wait_ge(scale_ready, b + 1)
                    take_m1(b, it, kk)
                    for n in banks[:1]:
                        high(b, it, n, blocks)
                    for q in t_banks(0):
                        t_high(b + 1, q)
                    for n in banks[1:]:
                        high(b, it, n, blocks)
                    for i in range(1, NP):
                        for q in t_banks(i):
                            t_high(b + 1, q)
                    if last and more and kk == BB - 1:
                        first_rows(b + 1, 0)
                        act.wait_ge(rstd_ready, b + 2)
                        take_y(b + 1, 0, 0)
                        first_rows(b + 1, 1)
                        take_y(b + 1, 0, 1)
                        high(b + 1, 0, 0, blocks - 1)
                        take_y(b + 1, 0, 2)
                        high(b + 1, 0, 1, blocks - 1)
                        first_rows(b + 1, 2)
                        high(b + 1, 0, 2, blocks - 1)
                    at = (number, kk) if more else None
                    if at == (0, 0):
                        load_om(b + 1)
                    if at == (0, 1):
                        load_xm(b + 1)
                    if at in ((0, 2), (0, 3)):
                        take_modes(b + 1, 2 * kk - 4)
                        take_modes(b + 1, 2 * kk - 3)
                    if at == (2, 2):
                        roots(b + 1)
                    if at == (NIT - 1, 0):
                        high_weights(b + 1)

            def image(b, more=True):
                body(b, 0, 0, more)
                body(b, 1, 1, more)
                body(b, 2, 2, more)
                with act.Fori(3, NIT - 1) as it:
                    body(b, it)
                body(b, NIT - 1, NIT - 1, more)

            load_om(0)
            load_xm(0)
            for q in range(NOT):
                take_modes(0, q)
            roots(0)
            high_weights(0)
            for q in range(NTB):
                t_high(0, q)
            for m in range(3):
                first_rows(0, m)
            act.wait_ge(rstd_ready, 1)
            act.wait_ge(cleared, 1)
            for n in range(NF):
                take_y(0, 0, n)
                high(0, 0, n, -1)
            with act.Fori(0, B - 1) as b:
                image(b)
            image(B - 1, more=False)

        @block.vector
        def _(dve):
            v = nc.vector

            def terms_rest(bn, step):
                dve.wait_ge(oc_evac, bn * NOT + NOT)
                dve.wait_ge(xm_in, bn * 16 + 16)
                step(v.tensor_tensor(col["dc"], oc[:, 0, 0:1], xm[:, 0, 0:1], ALU.add))
                step(v.scalar_tensor_tensor(xm[:, :, 1:], xm[:, :, 1:], 2.0, oc[:, :, 1:], ALU.mult, ALU.add))

            def sum_rest(bn, step):
                step(v.scalar_tensor_tensor(xm[:, :, 1:], xm[:, :, 1:], 1.0, oc[:, :, 1:], ALU.mult, ALU.mult,
                                            accum_out=col["a_rest"]))

            def sum_ky0(bn, step):
                step(v.scalar_tensor_tensor(xm[:, :, 0], xm[:, :, 0], 4.0, oc[:, :, 0], ALU.mult, ALU.add))
                step(v.scalar_tensor_tensor(xm[:, :, 0], xm[:, :, 0], 1.0, oc[:, :, 0], ALU.mult, ALU.mult,
                                            accum_out=col["a_ky0"]))
                step(v.scalar_tensor_tensor(xm[:, 1:32, 1], oc[:, 1:32, 0], 2.0, oc[:, 63:32:-1, 0],
                                            ALU.mult, ALU.mult, accum_out=col["a_mirror"]))
                step(v.tensor_tensor(col["a_dc"], oc[:, 0, 0:1], oc[:, 0, 0:1], ALU.mult))
                step(v.tensor_tensor(col["w1"], col["a_mirror"], col["a_dc"], ALU.add))
                step(v.tensor_tensor(col["w1"], col["w1"], con("sgnh"), ALU.mult))
                step(v.scalar_tensor_tensor(col["w2"], col["a_ky0"], 0.5, col["w1"], ALU.mult, ALU.add))
                step(v.scalar_tensor_tensor(col["part"], col["a_rest"], 2.0, col["w2"], ALU.mult, ALU.add))
                v.memset(sc[:, 47:48], 0.0).then_inc(part_ready, 1)

            def moments(bn, step):
                dve.wait_ge(group_done, bn + 1)
                step(v.tensor_scalar(col["mean_d"], ps[:, S0, 1:2], 1.0 / NORM, None, ALU.mult))
                step(v.tensor_tensor(col["mean"], col["mean_d"], mean0[:, bass.ds(bn, 1)], ALU.add))
                step(v.scalar_tensor_tensor(col["w1"], ps[:, S0, 0:1], 1.0 / NPIX, dev0[:, bass.ds(bn, 1)], ALU.mult, ALU.add))
                step(v.tensor_tensor(col["w2"], col["mean_d"], col["mean_d"], ALU.mult))
                step(v.scalar_tensor_tensor(col["w1"], col["w1"], 1.0 / NORM, col["w2"], ALU.mult, ALU.subtract))
                step(v.tensor_scalar(col["var"], col["w1"], 0.0, EPS, ALU.max, ALU.add))
                v.tensor_scalar(diag[:, :], con("diag_top"), col["mean"], None, ALU.mult).then_inc(mean_ready, 1)
                v.memset(sc[:, 47:48], 0.0).then_inc(var_ready, 1)

            def fix_modes(bn, step):
                dve.wait_ge(mrow_done, bn + 1)
                dve.wait_ge(bstep, step.before + step.n)
                step(v.tensor_copy(next_mrow[:, :], ps[:, S0 + 1, 0:C]))
                step(v.scalar_tensor_tensor(om[0:1, 0, 0, :], next_mrow[0:1, :], float(-NPIX), om[0:1, 0, 0, :], ALU.mult, ALU.add))
                step(v.scalar_tensor_tensor(om[NKX:NKX + 1, 1, 0, :], next_mrow[NKX:NKX + 1, :], float(NPIX),
                                            om[NKX:NKX + 1, 1, 0, :], ALU.mult, ALU.add))
                v.memset(sc[:, 47:48], 0.0).then_inc(om_fixed, 1)
                dve.wait_ge(sig_done, bn + 1)
                step(v.tensor_tensor(col["fro"], ps[:, S0, 2:3], w_sq[:, :], ALU.add))
                v.memset(sc[:, 47:48], 0.0).then_inc(fro_ready, 1)

            def scales(bn, step):
                dve.wait_ge(sd_ready, bn + 1)
                step(v.reciprocal(col["w1"], col["sd"]))
                step(v.tensor_tensor(col["w1"], col["w1"], col["var"], ALU.mult))
                step(v.tensor_tensor(col["w1"], col["w1"], col["sd"], ALU.add))
                step(v.tensor_scalar(col["sigma"], col["w1"], 0.5, None, ALU.mult))
                step(v.reciprocal(col["next_rstd"], col["sigma"]))
                dve.wait_ge(froot_ready, bn + 1)
                step(v.reciprocal(col["w2"], col["froot"]))
                step(v.tensor_scalar(col["f"], col["w2"], WSCALE, None, ALU.mult))
                step(v.reciprocal(col["next_inv_f"], col["f"]))
                step(v.tensor_scalar(col["next_neg_inv_f"], col["next_inv_f"], -1.0, None, ALU.mult))
                step(v.scalar_tensor_tensor(col["sigma_f"], col["sigma"], 0.5, col["f"], ALU.mult, ALU.mult))
                v.memset(sc[:, 47:48], 0.0).then_inc(f_ready, 1)

            def weights(bn, step):
                if not isinstance(bn, int):
                    dve.wait_ge(wl_ready, bn)
                flat = lambda t: t[:, :, :, :].rearrange("p a q o -> p (a q o)")
                dve.wait_ge(next_wh_ready, bn + 1)
                step(v.scalar_tensor_tensor(flat(next_wl), flat(taps), col["f"], flat(next_wh), ALU.mult, ALU.subtract))

            def centre(bn, step):
                for r in range(2):
                    half = slice(C * r, C * r + C)
                    v.tensor_scalar(wc[half, :, :], taps[half, 2:4, 1 + r, :], col["f"][half], None, ALU.mult)
                step(v.memset(sc[:, 47:48], 0.0))
                wide = con("diag2").unsqueeze(1).broadcast_to([P, 2, C])
                step(v.scalar_tensor_tensor(wc[:, :, :], wide, col["sigma_f"], wc[:, :, :], ALU.mult, ALU.add))
                for r in range(2):
                    half = slice(C * r, C * r + C)
                    v.tensor_copy(next_wh[half, 2:4, 1 + r, :], wc[half, :, :])
                step(v.memset(sc[:, 47:48], 0.0))
                for r in range(2):
                    half = slice(C * r, C * r + C)
                    v.tensor_tensor(next_wl[half, 2:4, 1 + r, :], wc[half, :, :], next_wh[half, 2:4, 1 + r, :], ALU.subtract)
                step(v.memset(sc[:, 47:48], 0.0))
                step.end()
                v.memset(sc[:, 47:48], 0.0).then_inc(next_ready, 1)

            def t_low(bn, q):
                dve.wait_ge(t_hi, bn * NTB + (q + 1))
                for half in range(2):
                    c = 2 * q + half * (C // 2)
                    mine, other = slice(64 * half, 64 * half + 64), slice(64 * (1 - half), 64 * (1 - half) + 64)
                    last = v.tensor_tensor(th[other, :, c:c + 2],
                                           ps[mine, S0 + q % t_banks_of(bn), :].rearrange("p (c h) -> p h c", c=2),
                                           th[mine, :, c:c + 2].bitcast(F32), ALU.subtract)
                last.then_inc(t_lo, 1)

            def switch_rstd(bn):
                dve.wait_ge(next_ready, bn + 1)
                dve.wait_ge(y_evac, bn * NY + YE)
                v.tensor_copy(col["rstd"], col["next_rstd"]).then_inc(rstd_ready, 1)

            def switch_weights(b):
                dve.wait_ge(next_ready, b + 1)
                dve.wait_ge(conv_done, b * (NP * NB) + CG)
                v.tensor_copy(wh[:, :, :, :].rearrange("p a q o -> p (a q o)"),
                              next_wh[:, :, :, :].rearrange("p a q o -> p (a q o)")).then_inc(wh_ready, 1)

            def switch_scales(b):
                dve.wait_ge(out_evac, b * (NV * NB) + NV)
                v.tensor_copy(col["inv_f"], col["next_inv_f"])
                v.tensor_copy(col["neg_inv_f"], col["next_neg_inv_f"])
                v.tensor_copy(mrow[:, :], next_mrow[:, :]).then_inc(scale_ready, 1)
                dve.wait_ge(scale_ready, b + 1)

            def sums(b, it, n):
                dve.wait_ge(y_evac, b * NY + it * (2 * BB) + (n + 1 + YE))
                dve.wait_ge(z_lo, b * NY + it * (2 * BB) + (n + 1))
                even, odd = yb[:, n % 2, :, 1 + PH:1 + W], yb[:, n % 2, :, 1:1 + PH]
                v.tensor_tensor(vb[:, n % 4, :, 2, :], even, odd, ALU.add)
                v.tensor_tensor(vb[:, n % 4, :, 3, :], even, odd, ALU.subtract).then_inc(v_sum, 1)

            def low(b, it, n):
                dve.wait_ge(z_hi, b * NY + it * (2 * BB) + (n + 1))
                v.tensor_tensor(z_slot(zl, n), v_slot(n), z_slot(zh, n), ALU.subtract).then_inc(z_lo, 1)

            def take(b, it, kk, i):
                blocks = b * NB + it * BB + kk
                dve.wait_ge(conv_done, blocks * NP + (i + 1) + CG)
                bank = ps[:, CV + i, :].rearrange("p (r o) -> p r o", o=C)
                start = m1[:, :].rearrange("p (r o) -> p r o", o=C)
                even, odd = ob[:, kk % OB, :, 0:C], ob[:, kk % OB, :, C:2 * C]
                if i == 1:
                    dve.wait_ge(out_stored[kk % OB], (b * (NB // OB) + it * (BB // OB) + kk // OB) * 16 + 16)
                    dve.wait_ge(m1_ready, blocks + 1)
                    v.scalar_tensor_tensor(even, bank, col["inv_f"], start, ALU.mult, ALU.add)
                    v.scalar_tensor_tensor(odd, bank, col["neg_inv_f"], start, ALU.mult, ALU.add).then_inc(out_evac, 1)
                else:
                    dve.wait_ge(out_evac, blocks * NV + NV + 1)
                    side, scale = ((even, col["inv_f"]), (odd, col["neg_inv_f"]))[i - 2]
                    v.scalar_tensor_tensor(side, bank, scale, side, ALU.mult, ALU.add).then_inc(out_evac, 1)

            def body(b, it, number=None, step=None, after_image=True):
                last = number == NIT - 1
                for kk, banks in enumerate(y_order(last)):
                    t_banks = lambda i: T_AT.get((kk, i), ()) if last and step else ()
                    new_image = number == 0 and kk == 0
                    before = (b - 1, NIT - 1, BB - 1) if new_image else (b, it - 1 if kk == 0 else it, (kk - 1) % BB)
                    if new_image:
                        switch_weights(b)
                        if after_image:
                            take(*before, 1)
                    if after_image or not new_image:
                        take(*before, 2)
                    if last and step and kk == BB - 1:
                        switch_rstd(b + 1)
                        sums(b + 1, 0, 0)
                        sums(b + 1, 0, 1)
                    for n in banks[:1]:
                        sums(b, it, n)
                    if after_image or not new_image:
                        take(*before, 3)
                    if new_image:
                        switch_scales(b)
                    for n in banks[1:]:
                        sums(b, it, n)
                    if last and step and kk == BB - 1:
                        low(b + 1, 0, 0)
                        sums(b + 1, 0, 2)
                        low(b + 1, 0, 1)
                        low(b + 1, 0, 2)
                    for q in t_banks(-1):
                        t_low(b + 1, q)
                    for n in banks[:1]:
                        low(b, it, n)
                    for q in t_banks(0):
                        t_low(b + 1, q)
                    for n in banks[1:]:
                        low(b, it, n)
                    for i in range(1, NP):
                        for q in t_banks(i):
                            t_low(b + 1, q)
                        if i == 1 and not (last and kk == BB - 1):
                            take(b, it, kk, 1)
                    at = (number, kk) if step else None
                    for when, piece in (((0, 3), terms_rest), ((1, 1), sum_rest), ((1, 3), sum_ky0), ((2, 0), moments),
                                        ((2, 1), fix_modes), ((2, 3), scales), ((NIT - 1, 1), weights),
                                        ((NIT - 1, 2), centre)):
                        if at == when:
                            piece(b + 1, step)

            def image(b, more=True, after_image=True):
                step = Chain(dve, bstep, (b + 1) * STEPS, STEPS) if more else None
                body(b, 0, 0, step, after_image)
                body(b, 1, 1, step)
                body(b, 2, 2, step)
                with dve.Fori(3, NIT - 1) as it:
                    body(b, it)
                body(b, NIT - 1, NIT - 1, step)

            v.memset(sc[:, 46:47], 0.0).then_inc(y_done, YG)
            for i, (s, given) in enumerate(((t_done, GIVEN), (t_lo, GIVEN), (part_ready, GIVEN), (ts_ready, GIVEN),
                                            (conv_done, CG), (y_evac, YE), (out_evac, NV), (m1_evac, GIVEN),
                                            (z_lo, SLOT), (v_sum, SLOT), (v_diff, SLOT))):
                v.memset(sc[:, 32 + i:33 + i], 0.0).then_inc(s, given)
            v.memset(yb[:, :, :, 0:1], 0.0)
            v.memset(yb[:, :, :, 1 + W:], 0.0).then_inc(cleared, 1)
            step = Chain(dve, bstep, 0, STEPS)
            for piece in (terms_rest, sum_rest, sum_ky0, moments, fix_modes, scales, weights, centre):
                piece(0, step)
            for q in range(NTB):
                t_low(0, q)
            switch_rstd(0)
            for n in range(NF):
                sums(0, 0, n)
                low(0, 0, n)
            image(0, after_image=False)
            with dve.Fori(1, B - 1) as b:
                image(b)
            image(B - 1, more=False)
            for i in (1, 2, 3):
                take(B - 1, NIT - 1, BB - 1, i)

        @block.gpsimd
        def _(pool):
            def diffs(b, it, n):
                pool.wait_ge(y_evac, b * NY + it * (2 * BB) + (n + 1 + YE))
                pool.wait_ge(z_lo, b * NY + it * (2 * BB) + (n + 1))
                cols = yb[:, n % 2, :, :].rearrange("p k (g e) -> p k g e", g=2)
                nc.gpsimd.tensor_tensor(vb[:, n % 4, :, 0:2, :], cols[:, :, :, 0:PH], cols[:, :, :, 1:1 + PH], ALU.subtract)\
                    .then_inc(v_diff, 1)

            def add_mean(b, it, kk):
                pool.wait_ge(m1_evac, b * NB + it * BB + (kk + 1) + GIVEN)
                rows = m1[:, :].rearrange("p (r o) -> p r o", o=C)
                nc.gpsimd.tensor_tensor(rows, rows, mrow[:, :].unsqueeze(1).broadcast_to([P, RB, C]), ALU.add)\
                    .then_inc(m1_ready, 1)

            def body(b, it, first=False, last=False, more=True):
                for kk, banks in enumerate(y_order(last)):
                    for n in banks:
                        diffs(b, it, n)
                    if first and kk == 0:
                        pool.wait_ge(scale_ready, b + 1)
                    add_mean(b, it, kk)
                if last and more:
                    for n in range(NF):
                        diffs(b + 1, 0, n)

            def image(b, more=True):
                body(b, 0, first=True)
                with pool.Fori(1, NIT - 1) as it:
                    body(b, it)
                body(b, NIT - 1, last=True, more=more)

            for n in range(NF):
                diffs(0, 0, n)
            with pool.Fori(0, B - 1) as b:
                image(b)
            image(B - 1, more=False)


_INS = ["x", "L0_conv_w_pos_r", "L0_conv_w_pos_i", "L0_conv_w_neg_r", "L0_conv_w_neg_i", "L1_conv_kernels"]


def kernel(**inputs):
    import concourse.bacc as bacc
    from concourse.bass_utils import run_bass_kernel_spmd

    nc = bacc.Bacc("TRN2", target_bir_lowering=False, num_devices=1)
    arrays, args = {}, []
    for name in _INS:
        arrays[name] = np.ascontiguousarray(inputs[name])
    arrays["constants"] = constants()
    for name, a in arrays.items():
        args.append(nc.dram_tensor(name, a.shape, mybir.dt.from_np(a.dtype), kind="ExternalInput").ap())
    out = nc.dram_tensor("out", (B, H, W, C), F32, kind="ExternalOutput").ap()
    program(nc, *args, out)
    r = run_bass_kernel_spmd(nc, [arrays], core_ids=[0])
    return r.results[0]["out"]
```
